# Optimizing a Trainium2 kernel written in Bass

```python
import numpy as np
import jax
import jax.numpy as jnp

def _softmax(x, axis=-1):
    return jax.nn.softmax(x, axis=axis)

def _gelu(x):
    return jax.nn.gelu(x, approximate=True)

def _silu(x):
    return jax.nn.silu(x)

def _sigmoid(x):
    return jax.nn.sigmoid(x)

def _layernorm(x, axis=-1, eps=1e-05):
    m = jnp.mean(x, axis=axis, keepdims=True)
    v = jnp.var(x, axis=axis, keepdims=True)
    return (x - m) / jnp.sqrt(v + eps)

def _scatter_add(tgt, idx, src, axis=0):
    return tgt.at[idx].add(src)

def _segment_sum(src, seg, n):
    return jax.ops.segment_sum(src, seg, n)
kernel_name = 'mk_xattn_seq_d1_seqx_r4_1e6724'

def setup_inputs(seed: int=0):
    np.random.seed(seed)
    _w = jnp.asarray

    def _rec_inputs():
        import jax
        import jax.numpy as jnp
        _rk = jax.random.key(seed)
        x = 7.22e-05 + 1 * jax.random.normal(jax.random.fold_in(_rk, 1), (4, 1024, 256), jnp.float32)
        _lenS = 1024 - jax.random.randint(jax.random.fold_in(_rk, 7), (4,), 0, max(1, 1024 // 4) + 1, jnp.int32)
        _lenS2 = 77 - jax.random.randint(jax.random.fold_in(_rk, 8), (4,), 0, max(1, 77 // 4) + 1, jnp.int32)
        _ctx_1024P = jax.random.normal(jax.random.fold_in(_rk, 11), (4, 16, 256), jnp.float32)
        _ctx_1024c = jax.random.dirichlet(jax.random.fold_in(_rk, 511), 0.3 * jnp.ones((16,), jnp.float32), (4, 77))
        _ctx_1024t = jnp.einsum('bsk,bkd->bsd', _ctx_1024c, _ctx_1024P)
        _ctx_1024t = _ctx_1024t * jax.lax.rsqrt(jnp.mean(jnp.square(_ctx_1024t)) + 1e-12) * 0.953939
        ctx_1024 = 4.13588e-05 + 0.999923 * (_ctx_1024t + 0.3 * jax.random.normal(jax.random.fold_in(_rk, 611), (4, 77, 256), jnp.float32))
        _validS = jnp.arange(1024)[None, :] < _lenS[:, None]
        _validS2 = jnp.arange(77)[None, :] < _lenS2[:, None]
        _causal = jnp.tril(jnp.ones((1024, 1024), dtype=bool))
        mask_BxSxS2_ik1 = jnp.where(jnp.broadcast_to(_validS2[:, None, :], (4, 1024, 77)), 1, 0).astype(jnp.int32)
        return (x, ctx_1024, mask_BxSxS2_ik1)
    x, ctx_1024, mask_BxSxS2_ik1 = _rec_inputs()

    def _L0_xattn_setup():
        import jax, jax.numpy as jnp
        import numpy as np
        D_MODEL = 256
        N_HEAD = 16
        D_K = D_MODEL // N_HEAD
        LN_EPS = 1e-05

        def _split_heads(x, W):
            B, S, _ = x.shape
            y = jnp.einsum('bsd,ed->bse', x, W)
            return y.reshape(B, S, N_HEAD, D_K).transpose(0, 2, 1, 3)
        key = jax.random.key(seed)
        ks = jax.random.split(key, 9)
        B, S = (4, 512)
        scale = 1.0 / np.sqrt(D_MODEL)
        return {'query': jax.random.normal(ks[0], (B, S, D_MODEL), jnp.float32), 'key': jax.random.normal(ks[1], (B, S, D_MODEL), jnp.float32), 'value': jax.random.normal(ks[2], (B, S, D_MODEL), jnp.float32), 'mask': jax.random.randint(ks[3], (B, S, S), 0, 2, jnp.int32), 'W_Q': jax.random.normal(ks[4], (D_MODEL, D_MODEL), jnp.float32) * scale, 'W_K': jax.random.normal(ks[5], (D_MODEL, D_MODEL), jnp.float32) * scale, 'W_V': jax.random.normal(ks[6], (D_MODEL, D_MODEL), jnp.float32) * scale, 'W_O': jax.random.normal(ks[7], (D_MODEL, D_MODEL), jnp.float32) * scale, 'gamma': jnp.ones((D_MODEL,), jnp.float32), 'beta': jnp.zeros((D_MODEL,), jnp.float32)}
    _L0_xattn_all = _L0_xattn_setup()
    _L0_xattn_in = {k: v for k, v in _L0_xattn_all.items() if k in ('W_Q', 'W_K', 'W_V', 'W_O', 'gamma', 'beta')}
    del _L0_xattn_all
    return {'x': x, 'ctx_1024': ctx_1024, 'mask_BxSxS2_ik1': mask_BxSxS2_ik1, 'L0_xattn_W_Q': _L0_xattn_in['W_Q'], 'L0_xattn_W_K': _L0_xattn_in['W_K'], 'L0_xattn_W_V': _L0_xattn_in['W_V'], 'L0_xattn_W_O': _L0_xattn_in['W_O'], 'L0_xattn_gamma': _L0_xattn_in['gamma'], 'L0_xattn_beta': _L0_xattn_in['beta']}

def reference(x, ctx_1024, mask_BxSxS2_ik1, L0_xattn_W_Q, L0_xattn_W_K, L0_xattn_W_V, L0_xattn_W_O, L0_xattn_gamma, L0_xattn_beta):
    import jax
    import jax.numpy as jnp

    def _L0_xattn_ref(query, key, value, mask, W_Q, W_K, W_V, W_O, gamma, beta):
        import jax, jax.numpy as jnp
        import numpy as np
        D_MODEL = 256
        N_HEAD = 16
        D_K = D_MODEL // N_HEAD
        LN_EPS = 1e-05

        def _split_heads(x, W):
            B, S, _ = x.shape
            y = jnp.einsum('bsd,ed->bse', x, W)
            return y.reshape(B, S, N_HEAD, D_K).transpose(0, 2, 1, 3)
        residual = query
        B, S, _ = query.shape
        q = _split_heads(query, W_Q)
        k = _split_heads(key, W_K)
        v = _split_heads(value, W_V)
        scores = jnp.einsum('bhqd,bhkd->bhqk', q, k) / np.sqrt(D_K)
        scores = jnp.where(mask[:, None, :, :] == 1, jnp.float32(-1000000000.0), scores)
        p = jax.nn.softmax(scores, axis=-1)
        ctx = jnp.einsum('bhqk,bhkd->bhqd', p, v)
        concat = ctx.transpose(0, 2, 1, 3).reshape(B, S, D_MODEL)
        out = jnp.einsum('bsd,ed->bse', concat, W_O) + residual
        mu = jnp.mean(out, axis=-1, keepdims=True)
        var = jnp.mean((out - mu) ** 2, axis=-1, keepdims=True)
        return (out - mu) * jax.lax.rsqrt(var + LN_EPS) * gamma + beta
    x = _L0_xattn_ref(x, ctx_1024, ctx_1024, mask_BxSxS2_ik1, L0_xattn_W_Q, L0_xattn_W_K, L0_xattn_W_V, L0_xattn_W_O, L0_xattn_gamma, L0_xattn_beta)
    return x

_drawn_inputs = setup_inputs


def setup_inputs(seed=0):
    import zlib

    import numpy as np

    out = dict(_drawn_inputs(seed))
    spreads = {'L0_xattn_gamma': (1.0, 0.2), 'L0_xattn_beta': (0.0, 0.1)}
    factors = {}
    for name, (base, spread) in spreads.items():
        noise = np.random.default_rng([zlib.crc32(name.encode()), seed]).standard_normal(out[name].shape)
        drawn = base * np.exp(spread * noise) if base else spread * noise
        out[name] = jnp.asarray(drawn.astype(out[name].dtype))
    for name, factor in factors.items():
        out[name] = (out[name] * factor).astype(out[name].dtype)
    return out
```

```python
from contextlib import ExitStack

import concourse.bass as bass
from concourse import mybir

F32 = mybir.dt.float32
F16 = mybir.dt.float16
I32 = mybir.dt.int32
ALU = mybir.AluOpType
ACT = mybir.ActivationFunctionType
AX = mybir.AxisListType

P = 128
BATCH = 4
SEQ = 1024
D = 256
HEADS = 16
DK = D // HEADS
KEYS = 77
EPS = 1e-5
BLOCK = 512
BLOCKS = BATCH * SEQ // BLOCK
TILES = BLOCK // P
HALVES = D // P
PAIRS = HEADS // 2
STEPS = PAIRS
QROWS = 3 * DK
MASK_ROW = QROWS
MAX_ROW = MASK_ROW + KEYS
KROWS = MAX_ROW + 1
BIG = 32768.0
GROUPS = [(0, 6), (6, 12), (12, 16)]
UNITS = len(GROUPS) * TILES
UNITS_AT = [2, 2, 3, 3, 2, 0, 0, 0]
UNIT_START = [sum(UNITS_AT[:s]) for s in range(STEPS)]
RLOADS = 4
KSCALE = 1.0 / float(DK) ** 0.5


def cross_attention(nc, x, ctx_in, mask, w_q, w_k, w_v, w_o, gamma, beta, out):
    stack = ExitStack()
    with stack:
        def sb(name, shape, dt=F32):
            return stack.enter_context(nc.sbuf_tensor(name, shape, dt))

        def ps(name, shape, dt=F32):
            return stack.enter_context(nc.psum_tensor(name, shape, dt))

        def sem(name):
            return stack.enter_context(nc.semaphore(name))

        q_scratch = [nc.dram_tensor(f"q_scratch{i}", [2, D, BLOCK], F16, kind="Internal").ap() for i in range(2)]
        k_scratch = nc.dram_tensor("k_scratch", [2, D, BATCH, KEYS], F16, kind="Internal").ap()

        x_all = sb("x_all", [P, BLOCKS * TILES, D])
        mask_all = sb("mask_all", [P, BLOCKS * TILES, KEYS], I32)
        w_in = [sb(f"w_in{i}", [P, HALVES, D]) for i in range(4)]
        w_t = [sb(f"w_t{i}", [P, HALVES, D]) for i in range(4)]
        ctx_sb = sb("ctx_sb", [KEYS, BATCH, D])
        ctx_t = sb("ctx_t", [P, HALVES, BATCH * KEYS])
        k16 = sb("k16", [P, 2, HALVES, BATCH * KEYS], F16)
        kb_all = sb("kb_all", [QROWS, BATCH, HEADS, KEYS], F16)
        kb_scores = sb("kb_scores", [KROWS, HEADS, KEYS], F16)
        kb_max = sb("kb_max", [KROWS, HEADS, KEYS], F16)
        kb_tail = sb("kb_tail", [KEYS + 1, HEADS, KEYS], F16)
        v_all = sb("v_all", [P, BATCH, HEADS, 32])
        v_now = sb("v_now", [P, HEADS, 32])
        ident = sb("ident", [P, P])
        ident16 = sb("ident16", [P, P], F16)
        gamma_sb = sb("gamma_sb", [P, D])
        beta_sb = sb("beta_sb", [P, D])
        minus_half = sb("minus_half", [P, TILES])
        mask_eq = sb("mask_eq", [P, TILES, KEYS])
        all_masked = sb("all_masked", [P, TILES])
        not_full = sb("not_full", [P, TILES])
        not_full_big = sb("not_full_big", [P, TILES])
        mask16 = sb("mask16", [P, TILES, KEYS], F16)
        mask_t = [sb(f"mask_t{i}", [KEYS, BLOCK], F16) for i in range(2)]
        xs = sb("xs", [P, TILES, D])
        x_t = sb("x_t", [P, HALVES, BLOCK])
        q16 = sb("q16", [P, 2, HALVES, BLOCK], F16)
        R = [sb(f"R{i}", [KROWS, HEADS, BLOCK], F16) for i in range(2)]
        neg_max = sb("neg_max", [P, TILES, HEADS])
        neg_max_t = sb("neg_max_t", [HEADS, BLOCK], F16)
        probs = sb("probs", [P, PAIRS, 2, BLOCK])
        ctx_q = sb("ctx_q", [P, 2, BLOCK // 32, 32])
        rden = sb("rden", [P, 2, BLOCK // 32])
        ctx_n = sb("ctx_n", [P, HALVES, BLOCK // 32, 32])
        ctx_e = [sb(f"ctx_e{i}", [P, HALVES, BLOCK]) for i in range(2)]
        y = [sb(f"y{i}", [P, TILES, D]) for i in range(2)]
        bn = sb("bn", [P, TILES, 6])
        mean_var = sb("mean_var", [P, TILES, 2])
        var_eps = sb("var_eps", [P, TILES])
        rstd = sb("rstd", [P, TILES])

        scores_ps = [ps(f"scores_ps{i}", [P, 2, BLOCK]) for i in range(2)]
        max_ps = [ps(f"max_ps{i}", [P, BLOCK]) for i in range(2)]
        pv_ps = ps("pv_ps", [P, BLOCK])
        work_ps = ps("work_ps", [P, BLOCK])
        work16 = work_ps[:, :].bitcast(F16)

        s_w = [sem(f"s_w{i}") for i in range(4)]
        s_ctx = sem("s_ctx")
        s_gb = sem("s_gb")
        s_x = [sem(f"s_x{i}") for i in range(BLOCKS)]
        s_mask = [sem(f"s_mask{i}") for i in range(2)]
        s_ident = sem("s_ident")
        s_zero = sem("s_zero")
        s_setup = sem("s_setup")
        w_t_done, w_t_ready = sem("w_t_done"), sem("w_t_ready")
        c_t_done, c_t_ready = sem("c_t_done"), sem("c_t_ready")
        k_done, k_high, k_low = sem("k_done"), sem("k_high"), sem("k_low")
        v_done, v_ready, v_ones = sem("v_done"), sem("v_ready"), sem("v_ones")
        s_k_out = sem("s_k_out")
        s_kb = sem("s_kb")
        tail_ready, s_tail = sem("tail_ready"), sem("s_tail")
        kb_scores_ready, kb_max_ready, v_now_ready = sem("kb_scores_ready"), sem("kb_max_ready"), sem("v_now_ready")
        eq_ready, full_ready, not_full_ready, mask16_ready = sem("eq_ready"), sem("full_ready"), sem("not_full_ready"), sem("mask16_ready")
        xs_ready = sem("xs_ready")
        mask_t_done, mask_t_ready = sem("mask_t_done"), sem("mask_t_ready")
        x_t_done, x_t_ready = sem("x_t_done"), sem("x_t_ready")
        q_done, q_high, q_low = sem("q_done"), sem("q_high"), sem("q_low")
        s_q_out = sem("s_q_out")
        s_R = [[sem(f"s_R{i}_{g}") for g in range(len(GROUPS))] for i in range(2)]
        max_done, max_reduced = sem("max_done"), sem("max_reduced")
        nm_done, nm_ready, s_nm = sem("nm_done"), sem("nm_ready"), sem("s_nm")
        scores_done, exp_done = sem("scores_done"), sem("exp_done")
        pv_done, pv_turned = sem("pv_done"), sem("pv_turned")
        rden_ready, ctx_normed, ctx_e_ready = sem("rden_ready"), sem("ctx_normed"), sem("ctx_e_ready")
        out_done, out_ready = sem("out_done"), sem("out_ready")
        y_ready, bn_ready, mv_ready, ve_ready, rstd_ready = sem("y_ready"), sem("bn_ready"), sem("mv_ready"), sem("ve_ready"), sem("rstd_ready")
        y_normed, y_gamma, y_beta = sem("y_normed"), sem("y_gamma"), sem("y_beta")
        s_store = [sem(f"s_store{i}") for i in range(2)]

        x_rows = x.rearrange("b (t p) d -> p (b t) d", p=P)
        mask_rows = mask.rearrange("b (t p) k -> p (b t) k", p=P)
        out_rows = out.rearrange("b (t p) d -> p (b t) d", p=P)

        block = stack.enter_context(nc.Block())

        def batches(eng, body):
            body(0, True, False)
            with eng.Fori(1, BATCH - 1) as b:
                body(b, False, False)
            body(BATCH - 1, False, True)

        def store_q(sp, m, par, b):
            sp.wait_ge(q_high, HALVES * (m + 1))
            sp.wait_ge(q_low, HALVES * (m + 1))
            if not isinstance(b, int) or b > 0:
                for g in range(len(GROUPS)):
                    sp.wait_ge(s_R[par][g], 16 * RLOADS * b)
            sp.dma_start(q_scratch[par].rearrange("l (t p) q -> p l t q", p=P), q16[:, :, :, :]).then_inc(s_q_out, 16)
            sp.wait_ge(s_q_out, 16 * (m + 1))
            sp.wait_ge(mask_t_ready, m + 1)

        def load_R(sp, m, par, b, g):
            lo, hi = GROUPS[g]
            for r, part in enumerate((0, 0, 1)):
                sp.dma_start(R[par][r * DK:(r + 1) * DK, lo:hi, :],
                             q_scratch[par][part, lo * DK:hi * DK, :].rearrange("(h d) q -> d h q", d=DK)
                             ).then_inc(s_R[par][g], 16)
            sp.dma_start(R[par][MASK_ROW:MAX_ROW, lo:hi, :],
                         mask_t[par][:, :].unsqueeze(1).to_broadcast([KEYS, hi - lo, BLOCK])).then_inc(s_R[par][g], 16)

        def store_out(sp, m, par, b):
            sp.wait_ge(y_beta, m + 1)
            dst = out_rows[:, bass.ds(m * TILES, TILES), :]
            sp.dma_start(dst, y[par][:, :, :]).then_inc(s_store[par], 16)

        @block.sync
        def _(sp):
            sp.dma_start(ctx_sb[:, :, :], ctx_in.rearrange("b k d -> k b d")).then_inc(s_ctx, 16)
            for i, w in enumerate((w_k, w_q)):
                sp.dma_start(w_in[i][:, :, :], w.rearrange("(t p) d -> p t d", p=P)).then_inc(s_w[i], 16)
            sp.dma_start(mask_all[:, 0:2 * TILES, :], mask_rows[:, 0:2 * TILES, :]).then_inc(s_mask[0], 16)
            for m in range(2):
                sp.dma_start(x_all[:, m * TILES:(m + 1) * TILES, :],
                             x_rows[:, m * TILES:(m + 1) * TILES, :]).then_inc(s_x[m], 16)
            for i, w in ((2, w_v), (3, w_o)):
                sp.dma_start(w_in[i][:, :, :], w.rearrange("(t p) d -> p t d", p=P)).then_inc(s_w[i], 16)
            sp.dma_start(mask_all[:, 2 * TILES:, :], mask_rows[:, 2 * TILES:, :]).then_inc(s_mask[1], 16)

            sp.wait_ge(tail_ready, 3)
            for kb in (kb_max, kb_scores):
                sp.dma_start(kb[MASK_ROW:KROWS, :, :], kb_tail[:, :, :]).then_inc(s_tail, 16)
            sp.wait_ge(k_high, HALVES)
            sp.wait_ge(k_low, HALVES)
            sp.dma_start(k_scratch.rearrange("l (t p) b k -> p l t (b k)", p=P), k16[:, :, :, :]).then_inc(s_k_out, 16)
            sp.wait_ge(s_k_out, 16)
            for r, part in enumerate((0, 1, 0)):
                for b in range(BATCH):
                    sp.dma_start(kb_all[r * DK:(r + 1) * DK, b, :, :],
                                 k_scratch[part, :, b, :].rearrange("(h d) k -> d h k", d=DK)).then_inc(s_kb, 16)
            for m in range(2):
                store_q(sp, m, m, 0)
                for g in range(len(GROUPS)):
                    load_R(sp, m, m, 0, g)
            for m in range(2, BLOCKS):
                sp.dma_start(x_all[:, m * TILES:(m + 1) * TILES, :],
                             x_rows[:, m * TILES:(m + 1) * TILES, :]).then_inc(s_x[m], 16)
            sp.dma_start(gamma_sb[:, :], gamma.rearrange("(a d) -> a d", a=1).to_broadcast([P, D])).then_inc(s_gb, 16)
            sp.dma_start(beta_sb[:, :], beta.rearrange("(a d) -> a d", a=1).to_broadcast([P, D])).then_inc(s_gb, 16)

            def body(b, first, last):
                for h in range(2):
                    n = 2 * b + h
                    if not first:
                        store_out(sp, n - 2, h, b - 1)
                    if not last:
                        store_q(sp, n + 2, h, b + 1)
                        for g in range(len(GROUPS)):
                            sp.wait_ge(scores_done, PAIRS * n + GROUPS[g][1] // 2)
                            load_R(sp, n + 2, h, b + 1, g)

            batches(sp, body)
            for h in range(2):
                store_out(sp, BLOCKS - 2 + h, h, BATCH - 1)
            for h in range(2):
                sp.wait_ge(s_store[h], 16 * BATCH)

        def pool_xs(pool, m, static):
            if static is not None:
                pool.wait_ge(s_x[static], 16)
            pool.wait_ge(not_full_ready, 2 * (m + 1))
            if static != 0:
                pool.wait_ge(x_t_done, HALVES * m)
            nc.gpsimd.tensor_tensor(xs[:, :, :], x_all[:, bass.ds(m * TILES, TILES), :],
                                    not_full[:, :].unsqueeze(2).to_broadcast([P, TILES, D]),
                                    ALU.mult).then_inc(xs_ready, 1)

        def pool_residual(pool, m, par):
            pool.wait_ge(out_ready, 2 * (m + 1))
            nc.gpsimd.tensor_tensor(y[par][:, :, :], y[par][:, :, :], x_all[:, bass.ds(m * TILES, TILES), :],
                                    ALU.add).then_inc(y_ready, 1)

        def pool_norm(pool, m, t):
            v, u = t // 2, t % 2
            pool.wait_ge(rden_ready, 4 * m + t + 1)
            if not (isinstance(m, int) and m == 0):
                pool.wait_ge(ctx_e_ready, 2 * (m - 1) + v + 1)
            nc.gpsimd.tensor_tensor(ctx_n[:, v, :, u * DK:(u + 1) * DK], ctx_q[:, t % 2, :, 0:DK],
                                    rden[:, t % 2, :].unsqueeze(2).to_broadcast([P, BLOCK // 32, DK]),
                                    ALU.mult).then_inc(ctx_normed, 1)

        def pool_rstd(pool, m):
            pool.wait_ge(ve_ready, 2 * (m + 1))
            nc.gpsimd.tensor_tensor(rstd[:, :], var_eps[:, :], minus_half[:, :], ALU.pow).then_inc(rstd_ready, 1)

        def pool_gamma(pool, m, par):
            pool.wait_ge(y_normed, m + 1)
            nc.gpsimd.tensor_tensor(y[par][:, :, :], y[par][:, :, :],
                                    gamma_sb[:, :].unsqueeze(1).to_broadcast([P, TILES, D]),
                                    ALU.mult).then_inc(y_gamma, 1)
            pool.wait_ge(y_gamma, m + 1)
            nc.gpsimd.tensor_tensor(y[par][:, :, :], y[par][:, :, :],
                                    beta_sb[:, :].unsqueeze(1).to_broadcast([P, TILES, D]),
                                    ALU.add).then_inc(y_beta, 1)

        @block.gpsimd
        def _(pool):
            pool.memset(ident[:, :], 0.0).then_inc(s_ident, 1)
            pool.wait_ge(s_ident, 1)
            pool.affine_select(out=ident[:, :], in_=ident[:, :], compare_op=ALU.not_equal, fill=1.0,
                               base=0, pattern=[[-1, P]], channel_multiplier=1).then_inc(s_ident, 1)
            pool.wait_ge(s_ident, 2)
            pool.tensor_copy(ident16[:, :], ident[:, :]).then_inc(s_ident, 1)
            pool.memset(minus_half[:, :], -0.5).then_inc(s_setup, 1)
            pool.memset(v_all[:, :, :, :], 0.0).then_inc(s_zero, 1)
            pool.wait_ge(s_zero, 1)
            pool.memset(v_all[0:KEYS, :, :, DK:DK + 1], 1.0).then_inc(v_ones, 1)
            for m in range(2):
                pool_xs(pool, m, m)

            def body(b, first, last):
                for h in range(2):
                    n = 2 * b + h
                    if first:
                        pool.wait_ge(s_x[n + 2], 16)
                    if first and h == 1:
                        for m in range(4, BLOCKS):
                            pool.wait_ge(s_x[m], 16)
                        pool.wait_ge(s_gb, 32)
                    if not last:
                        pool_xs(pool, n + 2, None)
                    if not first:
                        pool_residual(pool, n - 2, h)
                    if not (first and h == 0):
                        pool_norm(pool, n - 1, 2)
                        pool_norm(pool, n - 1, 3)
                    if not first:
                        pool_rstd(pool, n - 2)
                        pool_gamma(pool, n - 2, h)
                    pool_norm(pool, n, 0)
                    pool_norm(pool, n, 1)

            batches(pool, body)
            n = BLOCKS
            pool_residual(pool, n - 2, 0)
            pool_norm(pool, n - 1, 2)
            pool_norm(pool, n - 1, 3)
            pool_rstd(pool, n - 2)
            pool_gamma(pool, n - 2, 0)
            pool_residual(pool, n - 1, 1)
            pool_rstd(pool, n - 1)
            pool_gamma(pool, n - 1, 1)

        def act_mask_t(act, m, par, b):
            act.wait_ge(mask_t_done, m + 1)
            if not isinstance(b, int) or b > 0:
                for g in range(len(GROUPS)):
                    act.wait_ge(s_R[par][g], 16 * RLOADS * b)
            nc.scalar.activation(mask_t[par][:, :], work16[0:KEYS, 0:BLOCK], ACT.Copy).then_inc(mask_t_ready, 1)

        def act_x_t(act, m, t):
            act.wait_ge(x_t_done, HALVES * m + t + 1)
            if not (isinstance(m, int) and m == 0):
                act.wait_ge(q_done, HALVES * m)
            nc.scalar.activation(x_t[:, t, :], work_ps[:, :], ACT.Copy).then_inc(x_t_ready, 1)

        def act_q_high(act, m, e):
            act.wait_ge(q_done, HALVES * m + e + 1)
            if not (isinstance(m, int) and m == 0):
                act.wait_ge(s_q_out, 16 * m)
            nc.scalar.activation(q16[:, 0, e, :], work_ps[:, :], ACT.Copy).then_inc(q_high, 1)

        def act_nm(act, m, par):
            act.wait_ge(nm_done, m + 1)
            nc.scalar.activation(neg_max_t[:, :], work_ps[0:HEADS, :], ACT.Copy).then_inc(nm_ready, 1)
            act.wait_ge(nm_ready, m + 1)
            if not (isinstance(m, int) and m < 2):
                act.wait_ge(scores_done, PAIRS * (m - 1))
            act.dma_start(R[par][MAX_ROW:KROWS, :, :], neg_max_t[:, :]).then_inc(s_nm, 16)
            act.wait_ge(s_nm, 16 * (m + 1))

        def act_out(act, m, par, b, half):
            act.wait_ge(out_done, 2 * m + half + 1)
            if not isinstance(b, int) or b > 0:
                act.wait_ge(s_store[par], 16 * b)
            nc.scalar.activation(y[par][:, 2 * half:2 * half + 2, :], work_ps[:, :], ACT.Copy).then_inc(out_ready, 1)

        @block.scalar
        def _(act):
            for i in range(2):
                act.wait_ge(w_t_done, i + 1)
                nc.scalar.activation(w_t[i][:, :, :], scores_ps[i // 2][:, i % 2, :], ACT.Copy).then_inc(w_t_ready, 1)
            for e in range(HALVES):
                act.wait_ge(k_done, e + 1)
                nc.scalar.activation(k16[:, 0, e, :], (pv_ps, work_ps)[e][:, 0:BATCH * KEYS], ACT.Copy,
                                     scale=KSCALE).then_inc(k_high, 1)
            for i in range(2, 4):
                act.wait_ge(w_t_done, i + 1)
                nc.scalar.activation(w_t[i][:, :, :], scores_ps[i // 2][:, i % 2, :], ACT.Copy).then_inc(w_t_ready, 1)
            for m in range(2):
                act_mask_t(act, m, m, 0)
                for t in range(HALVES):
                    act_x_t(act, m, t)
                for t in range(HALVES):
                    act_q_high(act, m, t)
            for b in range(BATCH):
                act.wait_ge(v_done, b + 1)
                act.wait_ge(v_ones, 1)
                nc.scalar.activation(v_all[0:KEYS, b, :, 0:DK],
                                     scores_ps[b // 2][0:KEYS, b % 2, 0:D].rearrange("k (h d) -> k h d", d=DK),
                                     ACT.Copy).then_inc(v_ready, 1)
            act_nm(act, 0, 0)

            def body(b, first, last):
                for h in range(2):
                    n = 2 * b + h
                    for s in range(STEPS):
                        act.wait_ge(scores_done, PAIRS * n + s + 1)
                        if not (first and h == 0):
                            act.wait_ge(pv_done, 4 * (n - 1) + 2 * (s // 4) + 2)
                        nc.scalar.activation(probs[0:KEYS, s, :, :], scores_ps[s % 2][0:KEYS, :, :],
                                             ACT.Exp).then_inc(exp_done, 1)
                        if not last:
                            if s == 1:
                                act_mask_t(act, n + 2, h, b + 1)
                            if s in (2, 3):
                                act_x_t(act, n + 2, s - 2)
                            if s in (4, 5):
                                act_q_high(act, n + 2, s - 4)
                        if s == 6 and not (last and h == 1):
                            act_nm(act, n + 1, 1 - h)
                        if s in (6, 7) and not (first and h == 0):
                            act_out(act, n - 1, 1 - h, b - 1 if h == 0 else b, s - 6)

            batches(act, body)
            for half in range(2):
                act_out(act, BLOCKS - 1, 1, BATCH - 1, half)

        def dve_mask(dve, m, part):
            if part is not None:
                dve.wait_ge(s_mask[part], 16)
            if not (isinstance(m, int) and m == 0):
                dve.wait_ge(mask_t_done, m)
                dve.wait_ge(xs_ready, m)
                dve.wait_ge(mask16_ready, m)
            nc.vector.tensor_scalar(mask_eq[:, :, :], mask_all[:, bass.ds(m * TILES, TILES), :], 1.0, None,
                                    ALU.is_equal).then_inc(eq_ready, 1)
            dve.wait_ge(eq_ready, m + 1)
            nc.vector.tensor_reduce(all_masked[:, :], mask_eq[:, :, :], AX.X, ALU.min).then_inc(full_ready, 1)
            dve.wait_ge(full_ready, m + 1)
            nc.vector.tensor_scalar(not_full_big[:, :], all_masked[:, :], -BIG, BIG, ALU.mult, ALU.add).then_inc(not_full_ready, 1)
            nc.vector.tensor_scalar(not_full[:, :], all_masked[:, :], -1.0, 1.0, ALU.mult, ALU.add).then_inc(not_full_ready, 1)
            dve.wait_ge(not_full_ready, 2 * (m + 1))
            nc.vector.tensor_tensor(mask16[:, :, :], mask_eq[:, :, :],
                                    not_full_big[:, :].unsqueeze(2).to_broadcast([P, TILES, KEYS]),
                                    ALU.mult).then_inc(mask16_ready, 1)

        def dve_q_low(dve, m, e):
            dve.wait_ge(q_high, HALVES * m + e + 1)
            nc.vector.tensor_tensor(q16[:, 1, e, :], work_ps[:, :], q16[:, 0, e, :], ALU.subtract).then_inc(q_low, 1)

        def dve_max(dve, m, u):
            (lo, hi), t = GROUPS[u // TILES], u % TILES
            dve.wait_ge(max_done, UNITS * m + u + 1)
            if u == 0 and not (isinstance(m, int) and m == 0):
                dve.wait_ge(nm_done, m)
            nc.vector.tensor_reduce(neg_max[:, t, lo:hi],
                                    max_ps[u % 2][:, 0:(hi - lo) * KEYS].rearrange("p (h k) -> p h k", k=KEYS),
                                    AX.X, ALU.max, negate=True).then_inc(max_reduced, 1)

        def dve_turn(dve, m, t):
            dve.wait_ge(pv_done, 4 * m + t + 1)
            if not (isinstance(m, int) and m == 0 and t < 2):
                dve.wait_ge(ctx_normed, 4 * m + t - 1)
            nc.vector.transpose(ctx_q[:, t % 2, :, :], pv_ps[:, :]).then_inc(pv_turned, 1)
            dve.wait_ge(pv_turned, 4 * m + t + 1)
            nc.vector.reciprocal(rden[:, t % 2, :], ctx_q[:, t % 2, :, DK]).then_inc(rden_ready, 1)

        def dve_ctx_e(dve, m, v, par):
            dve.wait_ge(ctx_normed, 4 * m + 2 * v + 2)
            if not (isinstance(m, int) and m < 2):
                dve.wait_ge(out_done, 2 * (m - 1))
            nc.vector.transpose(ctx_e[par][:, v, :], ctx_n[:, v, :, :]).then_inc(ctx_e_ready, 1)

        def dve_stats(dve, m, par):
            dve.wait_ge(y_ready, m + 1)
            for t in range(TILES):
                if t > 0:
                    dve.wait_ge(bn_ready, TILES * m + t)
                nc.vector.bn_stats(bn[:, t, :], y[par][:, t, :]).then_inc(bn_ready, 1)
                if t > 0:
                    nc.vector.bn_aggr(mean_var[:, t - 1, :], bn[:, t - 1, :]).then_inc(mv_ready, 1)
            dve.wait_ge(bn_ready, TILES * (m + 1))
            dve.wait_ge(mv_ready, TILES * (m + 1) - 1)
            nc.vector.tensor_scalar(var_eps[:, 0:TILES - 1], mean_var[:, 0:TILES - 1, 1], EPS, None, ALU.add).then_inc(ve_ready, 1)
            nc.vector.bn_aggr(mean_var[:, TILES - 1, :], bn[:, TILES - 1, :]).then_inc(mv_ready, 1)
            dve.wait_ge(mv_ready, TILES * (m + 1))
            nc.vector.tensor_scalar(var_eps[:, TILES - 1:TILES], mean_var[:, TILES - 1:TILES, 1], EPS, None, ALU.add).then_inc(ve_ready, 1)

        def dve_apply(dve, m, par):
            dve.wait_ge(rstd_ready, m + 1)
            for t in range(TILES):
                last = nc.vector.tensor_scalar(y[par][:, t, :], y[par][:, t, :], mean_var[:, t, 0:1], rstd[:, t:t + 1],
                                               ALU.subtract, ALU.mult)
            last.then_inc(y_normed, 1)

        @block.vector
        def _(dve):
            dve_mask(dve, 0, 0)
            for t in range(HALVES):
                dve.wait_ge(c_t_done, t + 1)
                nc.vector.tensor_copy(ctx_t[:, t, :], max_ps[t][:, 0:BATCH * KEYS]).then_inc(c_t_ready, 1)
            nc.vector.memset(kb_tail[:, :, :], 1.0).then_inc(tail_ready, 1)
            dve.wait_ge(s_ident, 3)
            dve.wait_ge(tail_ready, 1)
            nc.vector.tensor_scalar(kb_tail[0:KEYS, 0, :], ident[0:KEYS, 0:KEYS], -BIG, None, ALU.mult).then_inc(tail_ready, 1)
            dve.wait_ge(tail_ready, 2)
            nc.vector.tensor_copy(kb_tail[0:KEYS, 1:HEADS, :],
                                  kb_tail[0:KEYS, 0, :].unsqueeze(1).to_broadcast([KEYS, HEADS - 1, KEYS])
                                  ).then_inc(tail_ready, 1)
            for e in range(HALVES):
                dve.wait_ge(k_high, e + 1)
                nc.vector.scalar_tensor_tensor(out=k16[:, 1, e, :], in0=(pv_ps, work_ps)[e][:, 0:BATCH * KEYS],
                                               scalar=KSCALE, in1=k16[:, 0, e, :],
                                               op0=ALU.mult, op1=ALU.subtract).then_inc(k_low, 1)
            dve_mask(dve, 1, 0)
            for s in range(PAIRS):
                nc.vector.memset(probs[64:P, s, :, :], 0.0).then_inc(s_zero, 1)
            for m in range(2):
                for e in range(HALVES):
                    dve_q_low(dve, m, e)
            dve.wait_ge(s_kb, 16 * 3 * BATCH)
            dve.wait_ge(s_tail, 32)
            nc.vector.tensor_copy(kb_max[0:QROWS, :, :], kb_all[:, 0, :, :]).then_inc(kb_max_ready, 1)
            for u in range(UNITS):
                dve_max(dve, 0, u)

            def body(b, first, last):
                for h in range(2):
                    n = 2 * b + h
                    if h == 0:
                        if not first:
                            dve.wait_ge(scores_done, PAIRS * n)
                        nc.vector.tensor_copy(kb_scores[0:QROWS, :, :], kb_all[:, bass.ds(b, 1), :, :].rearrange("p a h k -> p (a h) k")
                                              ).then_inc(kb_scores_ready, 1)
                    elif not last:
                        dve.wait_ge(max_done, UNITS * (n + 1))
                        nc.vector.tensor_copy(kb_max[0:QROWS, :, :], kb_all[:, bass.ds(b + 1, 1), :, :].rearrange("p a h k -> p (a h) k")
                                              ).then_inc(kb_max_ready, 1)
                    if first and h == 0:
                        dve.wait_ge(s_mask[1], 16)
                    if not last:
                        dve_mask(dve, n + 2, None)
                    for s in range(STEPS):
                        if not (last and h == 1):
                            for u in range(UNITS_AT[s]):
                                dve_max(dve, n + 1, UNIT_START[s] + u)
                        if not (first and h == 0):
                            if s in (1, 2):
                                dve_turn(dve, n - 1, s + 1)
                            if s == 3:
                                dve_ctx_e(dve, n - 1, 1, 1 - h)
                        if s == 3 and h == 0:
                            if not first:
                                dve.wait_ge(pv_done, 4 * n)
                            else:
                                dve.wait_ge(v_ready, BATCH)
                            nc.vector.tensor_copy(v_now[:, :, :], v_all[:, bass.ds(b, 1), :, :].rearrange("p a h k -> p (a h) k")
                                                  ).then_inc(v_now_ready, 1)
                        if s == 3 and not first:
                            dve_stats(dve, n - 2, h)
                        if s in (4, 5) and not last:
                            dve_q_low(dve, n + 2, s - 4)
                        if s == 5 and not first:
                            dve_apply(dve, n - 2, h)
                        if s in (6, 7):
                            dve_turn(dve, n, s - 6)
                        if s == 7:
                            dve_ctx_e(dve, n, 0, h)

            batches(dve, body)
            n = BLOCKS
            dve_turn(dve, n - 1, 2)
            dve_turn(dve, n - 1, 3)
            dve_ctx_e(dve, n - 1, 1, 1)
            dve_stats(dve, n - 2, 0)
            dve_apply(dve, n - 2, 0)
            dve_stats(dve, n - 1, 1)
            dve_apply(dve, n - 1, 1)

        def pe_scores(pe, m, s, par, b):
            if s == 0:
                pe.wait_ge(kb_scores_ready, b + 1)
                pe.wait_ge(s_nm, 16 * (m + 1))
            if not (isinstance(m, int) and m == 0 and s < 2):
                pe.wait_ge(exp_done, PAIRS * m + s - 1)
            for i in range(2):
                last = nc.tensor.matmul(scores_ps[s % 2][0:KEYS, i, :], kb_scores[:, 2 * s + i, :], R[par][:, 2 * s + i, :],
                                        start=True, stop=True)
            last.then_inc(scores_done, 1)

        def pe_max(pe, m, u, par, b):
            (lo, hi), t = GROUPS[u // TILES], u % TILES
            if u == 0:
                pe.wait_ge(kb_max_ready, b + 1)
            if t == 0:
                pe.wait_ge(s_R[par][u // TILES], 16 * RLOADS * (b + 1))
            if not (isinstance(m, int) and m == 0 and u < 2):
                pe.wait_ge(max_reduced, UNITS * m + u - 1)
            for i in range(hi - lo):
                last = nc.tensor.matmul(max_ps[u % 2][:, i * KEYS:(i + 1) * KEYS],
                                        R[par][0:MAX_ROW, lo + i, t * P:(t + 1) * P], kb_max[0:MAX_ROW, lo + i, :],
                                        start=True, stop=True)
            last.then_inc(max_done, 1)

        def pe_nm(pe, m):
            pe.wait_ge(max_reduced, UNITS * (m + 1))
            for t in range(TILES):
                last = nc.tensor.transpose(work_ps[0:HEADS, t * P:(t + 1) * P], neg_max[:, t, :], ident[:, :])
            last.then_inc(nm_done, 1)

        def pe_pv(pe, m, t, batches_ready):
            v, u = t // 2, t % 2
            if t == 0:
                pe.wait_ge(v_now_ready, batches_ready)
            pe.wait_ge(exp_done, PAIRS * m + 4 * (v + 1))
            if not (isinstance(m, int) and m == 0 and t == 0):
                pe.wait_ge(pv_turned, 4 * m + t)
            for j in range(4):
                last = nc.tensor.matmul(pv_ps[32 * j:32 * (j + 1), :], v_now[:, 8 * v + 2 * j + u, :],
                                        probs[:, 4 * v + j, u, :], start=True, stop=True)
            last.then_inc(pv_done, 1)

        def pe_mask_t(pe, m):
            pe.wait_ge(mask16_ready, m + 1)
            for t in range(TILES):
                last = nc.tensor.transpose(work16[0:KEYS, t * P:(t + 1) * P], mask16[:, t, :], ident16[:, :])
            last.then_inc(mask_t_done, 1)

        def pe_x_t(pe, m, d):
            if d == 0:
                pe.wait_ge(xs_ready, m + 1)
            for t in range(TILES):
                last = nc.tensor.transpose(work_ps[:, t * P:(t + 1) * P], xs[:, t, d * P:(d + 1) * P], ident[:, :])
            last.then_inc(x_t_done, 1)

        def pe_q(pe, m, e):
            pe.wait_ge(x_t_ready, HALVES * (m + 1))
            for t in range(HALVES):
                last = nc.tensor.matmul(work_ps[:, :], w_t[1][:, t, e * P:(e + 1) * P], x_t[:, t, :],
                                        start=(t == 0), stop=(t == HALVES - 1))
            last.then_inc(q_done, 1)

        def pe_out(pe, m, par, half):
            if half == 0:
                pe.wait_ge(ctx_e_ready, HALVES * (m + 1))
            for i in range(2):
                q0 = (2 * half + i) * P
                for v in range(HALVES):
                    last = nc.tensor.matmul(work_ps[:, i * D:(i + 1) * D], ctx_e[par][:, v, q0:q0 + P], w_t[3][:, v, :],
                                            start=(v == 0), stop=(v == HALVES - 1))
            last.then_inc(out_done, 1)

        @block.tensor
        def _(pe):
            pe.wait_ge(s_ident, 3)

            def turn_weight(i):
                pe.wait_ge(s_w[i], 16)
                for t in range(HALVES):
                    for e in range(HALVES):
                        last = nc.tensor.transpose(scores_ps[i // 2][:, i % 2, t * D + e * P:t * D + (e + 1) * P],
                                                   w_in[i][:, e, t * P:(t + 1) * P], ident[:, :])
                last.then_inc(w_t_done, 1)

            pe.wait_ge(s_ctx, 16)
            for t in range(HALVES):
                for b in range(BATCH):
                    last = nc.tensor.transpose(max_ps[t][:, b * KEYS:(b + 1) * KEYS], ctx_sb[:, b, t * P:(t + 1) * P],
                                               ident[0:KEYS, 0:KEYS])
                last.then_inc(c_t_done, 1)
            turn_weight(0)
            turn_weight(1)
            pe.wait_ge(c_t_ready, HALVES)
            pe.wait_ge(w_t_ready, 1)
            for e in range(HALVES):
                for t in range(HALVES):
                    last = nc.tensor.matmul((pv_ps, work_ps)[e][:, 0:BATCH * KEYS], w_t[0][:, t, e * P:(e + 1) * P],
                                            ctx_t[:, t, :], start=(t == 0), stop=(t == HALVES - 1))
                last.then_inc(k_done, 1)
            turn_weight(2)
            turn_weight(3)
            for m in range(2):
                if m == 0:
                    pe.wait_ge(k_low, HALVES)
                else:
                    pe.wait_ge(q_low, HALVES * m)
                pe_mask_t(pe, m)
                pe.wait_ge(mask_t_ready, m + 1)
                pe_x_t(pe, m, 0)
                pe.wait_ge(x_t_ready, HALVES * m + 1)
                pe_x_t(pe, m, 1)
                if m == 0:
                    pe.wait_ge(w_t_ready, 2)
                pe_q(pe, m, 0)
                pe.wait_ge(q_low, HALVES * m + 1)
                pe_q(pe, m, 1)
            pe.wait_ge(w_t_ready, 4)
            for b in range(BATCH):
                for t in range(HALVES):
                    last = nc.tensor.matmul(scores_ps[b // 2][0:KEYS, b % 2, 0:D], ctx_t[:, t, b * KEYS:(b + 1) * KEYS],
                                            w_t[2][:, t, :], start=(t == 0), stop=(t == HALVES - 1))
                last.then_inc(v_done, 1)
            for u in range(UNITS):
                pe_max(pe, 0, u, 0, 0)
            pe.wait_ge(q_low, 2 * HALVES)
            pe_nm(pe, 0)
            pe.wait_ge(v_ready, BATCH)
            pe.wait_ge(s_zero, 1 + PAIRS)

            def body(b, first, last):
                for h in range(2):
                    n = 2 * b + h
                    for s in range(STEPS):
                        pe_scores(pe, n, s, h, b)
                        if not (last and h == 1):
                            for u in range(UNITS_AT[s]):
                                pe_max(pe, n + 1, UNIT_START[s] + u, 1 - h, b + h)
                        if s in (1, 2) and not (first and h == 0):
                            pe_pv(pe, n - 1, s + 1, b + h)
                        if s in (5, 6):
                            pe_pv(pe, n, s - 5, b + 1)
                        if not last:
                            if s == 1:
                                if first:
                                    pe.wait_ge(nm_ready, n + 1)
                                else:
                                    pe.wait_ge(out_ready, 2 * (n - 1))
                                pe_mask_t(pe, n + 2)
                            if s == 2:
                                pe.wait_ge(mask_t_ready, n + 3)
                                pe_x_t(pe, n + 2, 0)
                            if s == 3:
                                pe.wait_ge(x_t_ready, HALVES * (n + 2) + 1)
                                pe_x_t(pe, n + 2, 1)
                            if s == 4:
                                pe_q(pe, n + 2, 0)
                            if s == 5:
                                pe.wait_ge(q_low, HALVES * (n + 2) + 1)
                                pe_q(pe, n + 2, 1)
                        if s == 6 and not (last and h == 1):
                            if not last:
                                pe.wait_ge(q_low, HALVES * (n + 3))
                            else:
                                pe.wait_ge(out_ready, 2 * (n - 1))
                            pe_nm(pe, n + 1)
                        if s in (6, 7) and not (first and h == 0):
                            if s == 6 and not (last and h == 1):
                                pe.wait_ge(nm_ready, n + 2)
                            elif s == 6:
                                pe.wait_ge(out_ready, 2 * (n - 1))
                            else:
                                pe.wait_ge(out_ready, 2 * (n - 1) + 1)
                            pe_out(pe, n - 1, 1 - h, s - 6)

            batches(pe, body)
            n = BLOCKS
            pe_pv(pe, n - 1, 2, BATCH)
            pe_pv(pe, n - 1, 3, BATCH)
            for half in range(2):
                pe.wait_ge(out_ready, 2 * (n - 1) + half)
                pe_out(pe, n - 1, 1, half)


_INS = ['x', 'ctx_1024', 'mask_BxSxS2_ik1', 'L0_xattn_W_Q', 'L0_xattn_W_K', 'L0_xattn_W_V', 'L0_xattn_W_O',
        'L0_xattn_gamma', 'L0_xattn_beta']


def kernel(**inputs):
    import numpy as np
    import concourse.bacc as bacc
    from concourse.bass_utils import run_bass_kernel_spmd

    nc = bacc.Bacc("TRN2", target_bir_lowering=False, num_devices=1)
    arrays, args = {}, []
    for name in _INS:
        a = np.ascontiguousarray(inputs[name])
        arrays[f"in_{name}"] = a
        args.append(nc.dram_tensor(f"in_{name}", a.shape, mybir.dt.from_np(a.dtype), kind="ExternalInput").ap())
    out = nc.dram_tensor("out", (BATCH, SEQ, D), F32, kind="ExternalOutput").ap()
    cross_attention(nc, *args, out)
    return run_bass_kernel_spmd(nc, [arrays], core_ids=[0]).results[0]["out"]
```

```python
from contextlib import ExitStack

import concourse.bass as bass
from concourse import mybir

F32 = mybir.dt.float32
F16 = mybir.dt.float16
I32 = mybir.dt.int32
ALU = mybir.AluOpType
ACT = mybir.ActivationFunctionType
AX = mybir.AxisListType

P = 128
BATCH = 4
SEQ = 1024
D = 256
HEADS = 16
DK = D // HEADS
KEYS = 77
EPS = 1e-5
BLOCK = 512
BLOCKS = BATCH * SEQ // BLOCK
TILES = BLOCK // P
HALVES = D // P
PAIRS = HEADS // 2
STEPS = PAIRS
QROWS = 3 * DK
MASK_ROW = QROWS
MAX_ROW = MASK_ROW + KEYS
KROWS = MAX_ROW + 1
BIG = 32768.0
GROUPS = [(0, 6), (6, 12), (12, 16)]
UNITS = len(GROUPS) * TILES
UNITS_AT = [2, 2, 2, 2, 2, 2, 0, 0]
UNIT_START = [sum(UNITS_AT[:s]) for s in range(STEPS)]
PV_AT = (1, 3, 5, 7)
NM_AT = 5
XT_AT = (0, 1)
Q_AT = (2, 3)
OUT_AT = (6, 7)
STATS_AT = (0, 1, 2, 3)
VARIANCE_AT = 5
APPLY_AT = (6, 7)
CTX_AT = (1, 5)
RLOADS = 3
GROUPS_OF = [[g for g, (lo, hi) in enumerate(GROUPS) if lo < (e + 1) * PAIRS and hi > e * PAIRS] for e in range(HALVES)]
MASK_PARTS = [(0, 1), (1, 2), (2, BLOCKS)]
MASK_TURNS = [(0, 1), (1, 2), (2, 4), (4, 6), (6, BLOCKS)]
KSCALE = 1.0 / float(DK) ** 0.5


def cross_attention(nc, x, ctx_in, mask, w_q, w_k, w_v, w_o, gamma, beta, out):
    stack = ExitStack()
    with stack:
        def sb(name, shape, dt=F32):
            return stack.enter_context(nc.sbuf_tensor(name, shape, dt))

        def ps(name, shape, dt=F32):
            return stack.enter_context(nc.psum_tensor(name, shape, dt))

        def sem(name):
            return stack.enter_context(nc.semaphore(name))

        q_scratch = [nc.dram_tensor(f"q_scratch{i}", [HEADS, 2, DK, BLOCK], F16, kind="Internal").ap() for i in range(2)]
        k_scratch = nc.dram_tensor("k_scratch", [2, HEADS, DK, BATCH * KEYS], F16, kind="Internal").ap()

        x_all = sb("x_all", [P, BLOCKS * TILES, D])
        mask_all = sb("mask_all", [P, BLOCKS * TILES, KEYS], I32)
        w_t = [sb(f"w_t{i}", [P, HALVES, D]) for i in range(4)]
        ctx_sb = sb("ctx_sb", [KEYS, BATCH, D])
        ctx_t = sb("ctx_t", [P, HALVES, BATCH * KEYS])
        k16 = sb("k16", [P, 2, HALVES, BATCH * KEYS], F16)
        kb_all = sb("kb_all", [QROWS, HEADS, BATCH * KEYS], F16)
        kb_scores = sb("kb_scores", [KROWS, HEADS, KEYS], F16)
        kb_max = sb("kb_max", [KROWS, HEADS, KEYS], F16)
        kb_tail = sb("kb_tail", [KEYS + 1, HEADS, KEYS], F16)
        v_all = sb("v_all", [P, BATCH, HEADS, 32])
        v_now = sb("v_now", [P, HEADS, 32])
        ident = sb("ident", [P, P])
        ident16 = sb("ident16", [P, P], F16)
        gamma_sb = sb("gamma_sb", [P, D])
        beta_sb = sb("beta_sb", [P, D])
        minus_half = sb("minus_half", [P, TILES])
        all_masked = sb("all_masked", [P, BLOCKS * TILES])
        not_full = sb("not_full", [P, BLOCKS * TILES])
        not_full_big = sb("not_full_big", [P, BLOCKS * TILES])
        mask16 = sb("mask16", [P, BLOCKS * TILES, KEYS], F16)
        mask_t = sb("mask_t", [KEYS, BLOCKS, BLOCK], F16)
        xs = sb("xs", [P, TILES, D])
        x_t = sb("x_t", [P, HALVES, BLOCK])
        q16 = sb("q16", [P, HALVES, 2, BLOCK], F16)
        R = [sb(f"R{i}", [KROWS, HEADS, BLOCK], F16) for i in range(2)]
        neg_max = sb("neg_max", [P, TILES, HEADS], F16)
        neg_max_t = sb("neg_max_t", [HEADS, BLOCK], F16)
        probs = sb("probs", [P, PAIRS, 2, BLOCK])
        spare = probs[:, 4:6, :, :].rearrange("p s i q -> p (s i q)").rearrange("p (i t d) -> p i t d", t=HALVES, d=D)
        w_in = [spare[:, i, :, :] for i in range(4)]
        mask_eq = probs[:, 6:8, :, :].rearrange("p s i q -> p (s i q)").bitcast(F16)[:, 0:BLOCKS * TILES * KEYS].rearrange(
            "p (t k) -> p t k", k=KEYS)
        ctx_q = sb("ctx_q", [P, 2, BLOCK // 32, 32])
        rden = sb("rden", [P, 2, BLOCK // 32])
        ctx_n = sb("ctx_n", [P, HALVES, BLOCK // 32, 32])
        ctx_e = [sb(f"ctx_e{i}", [P, HALVES, BLOCK]) for i in range(2)]
        y = [sb(f"y{i}", [P, TILES, D]) for i in range(2)]
        bn = sb("bn", [P, TILES, 6])
        mean_var = sb("mean_var", [P, TILES, 2])
        var_eps = sb("var_eps", [P, TILES])
        neg_mean = sb("neg_mean", [P, TILES])
        rstd = sb("rstd", [P, TILES])
        shift = sb("shift", [P, TILES])

        scores_ps = [ps(f"scores_ps{i}", [P, 2, BLOCK]) for i in range(2)]
        max_ps = [ps(f"max_ps{i}", [P, BLOCK]) for i in range(2)]
        pv_ps = ps("pv_ps", [P, BLOCK])
        work_ps = ps("work_ps", [P, BLOCK])
        work16 = work_ps[:, :].bitcast(F16)
        pv16 = pv_ps[:, :].bitcast(F16)
        scores16 = scores_ps[1][:, 0, :].bitcast(F16)
        max16 = [t[:, :].bitcast(F16) for t in max_ps]

        s_w = [sem(f"s_w{i}") for i in range(4)]
        s_ctx = sem("s_ctx")
        s_gb = sem("s_gb")
        s_x = [sem(f"s_x{i}") for i in range(BLOCKS)]
        s_mask = [sem(f"s_mask{i}") for i in range(2)]
        s_ident = sem("s_ident")
        s_zero = sem("s_zero")
        w_t_done, w_t_ready = sem("w_t_done"), sem("w_t_ready")
        c_t_done, c_t_ready = sem("c_t_done"), sem("c_t_ready")
        k_done, k_high, k_low = sem("k_done"), sem("k_high"), sem("k_low")
        v_done, v_ready, v_ones = sem("v_done"), sem("v_ready"), sem("v_ones")
        s_k_out = sem("s_k_out")
        s_kb = sem("s_kb")
        tail_ready, s_tail = sem("tail_ready"), sem("s_tail")
        kb_scores_ready, kb_max_ready, v_now_ready = sem("kb_scores_ready"), sem("kb_max_ready"), sem("v_now_ready")
        eq_ready, full_ready, not_full_ready, mask16_ready = sem("eq_ready"), sem("full_ready"), sem("not_full_ready"), sem("mask16_ready")
        xs_ready = sem("xs_ready")
        mask_t_done, mask_t_ready = sem("mask_t_done"), sem("mask_t_ready")
        x_t_done, x_t_ready = sem("x_t_done"), sem("x_t_ready")
        q_done, q_high, q_low = sem("q_done"), sem("q_high"), sem("q_low")
        s_q_out = [sem(f"s_q_out{e}") for e in range(HALVES)]
        s_R = [[sem(f"s_R{i}_{g}") for g in range(len(GROUPS))] for i in range(2)]
        max_done, max_reduced = sem("max_done"), sem("max_reduced")
        nm_done, nm_ready, s_nm = sem("nm_done"), sem("nm_ready"), sem("s_nm")
        scores_done, exp_done = sem("scores_done"), sem("exp_done")
        pv_done, pv_turned = sem("pv_done"), sem("pv_turned")
        rden_ready, ctx_normed, ctx_e_ready = sem("rden_ready"), sem("ctx_normed"), sem("ctx_e_ready")
        out_done, out_ready = sem("out_done"), sem("out_ready")
        bn_ready, mv_ready, ve_ready, rstd_ready, shift_ready = sem("bn_ready"), sem("mv_ready"), sem("ve_ready"), sem("rstd_ready"), sem("shift_ready")
        y_normed, y_gamma, y_beta = sem("y_normed"), sem("y_gamma"), sem("y_beta")
        y_last = sem("y_last")
        s_store = [sem(f"s_store{i}") for i in range(2)]

        x_rows = x.rearrange("b (m p t) d -> p (b m) t d", p=P, t=TILES)
        mask_rows = mask.rearrange("b (m p t) k -> p (b m) t k", p=P, t=TILES)
        out_rows = out.rearrange("b (m p t) d -> p (b m) t d", p=P, t=TILES)

        block = stack.enter_context(nc.Block())

        def batches(eng, body):
            body(0, True, False)
            with eng.Fori(1, BATCH - 1) as b:
                body(b, False, False)
            body(BATCH - 1, False, True)


        def store_q(sp, m, par, b, e):
            sp.wait_ge(q_low, HALVES * m + e + 1)
            if not isinstance(b, int) or b > 0:
                for g in GROUPS_OF[e]:
                    sp.wait_ge(s_R[par][g], 16 * RLOADS * b)
            for part in range(2):
                sp.dma_start(q_scratch[par][e * PAIRS:(e + 1) * PAIRS, part, :, :], q16[:, e, part, :]).then_inc(s_q_out[e], 16)

        def load_mask(sp, m, par, g):
            lo, hi = GROUPS[g]
            sp.dma_start(R[par][MASK_ROW:MAX_ROW, lo:hi, :],
                         mask_t[:, bass.ds(m, 1), :].to_broadcast([KEYS, hi - lo, BLOCK])).then_inc(s_R[par][g], 16)

        def load_q(sp, par, g):
            lo, hi = GROUPS[g]
            sp.dma_start(R[par][0:2 * DK, lo:hi, :], q_scratch[par][lo:hi, :, :, :].rearrange("h l d q -> (l d) h q")
                         ).then_inc(s_R[par][g], 16)
            sp.dma_start(R[par][2 * DK:3 * DK, lo:hi, :], q_scratch[par][lo:hi, 0, :, :].rearrange("h d q -> d h q")).then_inc(s_R[par][g], 16)

        def store_out(sp, m, par):
            sp.wait_ge(y_beta, m + 1)
            sp.dma_start(out_rows[:, bass.ds(m, 1), :, :].rearrange("p m t d -> p (m t) d"), y[par][:, :, :]).then_inc(s_store[par], 16)

        @block.sync
        def _(sp):
            def load_weight(i, w):
                sp.dma_start(w_in[i][:, :, :], w.rearrange("(t p) d -> p t d", p=P)).then_inc(s_w[i], 16)

            def load_x(m):
                sp.dma_start(x_all[:, m * TILES:(m + 1) * TILES, :],
                             x_rows[:, m, :, :]).then_inc(s_x[m], 16)

            load_weight(1, w_k)
            sp.dma_start(ctx_sb[:, :, :], ctx_in.rearrange("b k d -> k b d")).then_inc(s_ctx, 16)
            sp.dma_start(mask_all[:, 0:TILES, :], mask_rows[:, 0, :, :]).then_inc(s_mask[0], 16)
            load_x(0)
            load_weight(0, w_q)
            sp.wait_ge(tail_ready, 3)
            for kb in (kb_max, kb_scores):
                sp.dma_start(kb[MASK_ROW:KROWS, :, :], kb_tail[:, :, :]).then_inc(s_tail, 16)
            load_weight(2, w_v)
            load_x(1)
            sp.dma_start(mask_all[:, TILES:, :].rearrange("p (m t) k -> p m t k", t=TILES), mask_rows[:, 1:, :, :]).then_inc(s_mask[1], 16)
            sp.wait_ge(k_low, HALVES)
            sp.dma_start(k_scratch.rearrange("l (e h) d k -> (h d) (l e) k", e=HALVES), k16[:, :, :, :].rearrange("p l e k -> p (l e) k")
                         ).then_inc(s_k_out, 16)
            sp.wait_ge(mask_t_ready, 1)
            for g in range(len(GROUPS)):
                load_mask(sp, 0, 0, g)
            sp.wait_ge(s_k_out, 16)
            for lo, hi, parts in ((0, 1, k_scratch[0]), (1, 2, k_scratch[0]), (2, 3, k_scratch[1])):
                sp.dma_start(kb_all[lo * DK:hi * DK, :, :], parts.rearrange("h d k -> d h k")).then_inc(s_kb, 16)
            for e in range(HALVES):
                store_q(sp, 0, 0, 0, e)
            for g in range(len(GROUPS)):
                for e in range(HALVES):
                    if g == GROUPS_OF[e][0]:
                        sp.wait_ge(s_q_out[e], 32)
                load_q(sp, 0, g)
            load_weight(3, w_o)
            sp.dma_start(gamma_sb[:, :], gamma.rearrange("(a d) -> a d", a=1).to_broadcast([P, D])).then_inc(s_gb, 16)
            sp.dma_start(beta_sb[:, :], beta.rearrange("(a d) -> a d", a=1).to_broadcast([P, D])).then_inc(s_gb, 16)
            load_x(2)
            sp.wait_ge(mask_t_ready, 2)
            for g in range(len(GROUPS)):
                load_mask(sp, 1, 1, g)
            for e in range(HALVES):
                store_q(sp, 1, 1, 0, e)
            for g in range(len(GROUPS)):
                for e in range(HALVES):
                    if g == GROUPS_OF[e][0]:
                        sp.wait_ge(s_q_out[e], 64)
                load_q(sp, 1, g)
            sp.wait_ge(s_nm, 16)
            for m in range(3, 6):
                load_x(m)
            sp.wait_ge(mask_t_ready, len(MASK_TURNS))

            def body(b, first, last):
                for h in range(2):
                    n = 2 * b + h
                    if first:
                        load_x(6 + h)
                    if not last:
                        for e in range(HALVES):
                            store_q(sp, n + 2, h, b + 1, e)
                        for g in range(len(GROUPS)):
                            sp.wait_ge(scores_done, PAIRS * n + GROUPS[g][1] // 2)
                            for e in range(HALVES):
                                if g == GROUPS_OF[e][0]:
                                    sp.wait_ge(s_q_out[e], 32 * (n + 3))
                            load_q(sp, h, g)
                            load_mask(sp, n + 2, h, g)
                            if g == 1 and not first:
                                store_out(sp, n - 2, h)
                    elif h == 0:
                        store_out(sp, n - 2, h)

            batches(sp, body)
            store_out(sp, BLOCKS - 3, 1)
            store_out(sp, BLOCKS - 2, 0)
            for half in range(2):
                sp.wait_ge(y_last, half + 2)
                sp.dma_start(out_rows[:, BLOCKS - 1, 2 * half:2 * half + 2, :], xs[:, 2 * half:2 * half + 2, :]
                             ).then_inc(s_store[1], 16)
            sp.wait_ge(s_store[0], 16 * BATCH)
            sp.wait_ge(s_store[1], 16 * (BATCH + 1))


        def mask_product(maths, eng, part):
            t0, t1 = (i * TILES for i in MASK_PARTS[part])
            eng.wait_ge(not_full_ready, 2 * (part + 1))
            maths.tensor_tensor(mask16[:, t0:t1, :], mask_eq[:, t0:t1, :],
                                not_full_big[:, t0:t1].unsqueeze(2).to_broadcast([P, t1 - t0, KEYS]),
                                ALU.mult).then_inc(mask16_ready, 1)

        def pool_xs(pool, m):
            if m > 0:
                pool.wait_ge(x_t_done, HALVES * m)
            nc.gpsimd.tensor_tensor(xs[:, :, :], x_all[:, m * TILES:(m + 1) * TILES, :],
                                    not_full[:, m * TILES:(m + 1) * TILES].unsqueeze(2).to_broadcast([P, TILES, D]),
                                    ALU.mult).then_inc(xs_ready, TILES)

        def pool_norm(pool, m, t):
            v, u = t // 2, t % 2
            pool.wait_ge(rden_ready, 4 * m + t + 1)
            if not (isinstance(m, int) and m == 0):
                pool.wait_ge(ctx_e_ready, 2 * (m - 1) + v + 1)
            nc.gpsimd.tensor_tensor(ctx_n[:, v, :, u * DK:(u + 1) * DK], ctx_q[:, t % 2, :, 0:DK],
                                    rden[:, t % 2, :].unsqueeze(2).to_broadcast([P, BLOCK // 32, DK]),
                                    ALU.mult).then_inc(ctx_normed, 1)

        def pool_rstd(pool, m):
            pool.wait_ge(ve_ready, 3 * (m + 1))
            if not (isinstance(m, int) and m == 0):
                pool.wait_ge(y_normed, m)
            nc.gpsimd.tensor_tensor(rstd[:, :], var_eps[:, :], minus_half[:, :], ALU.pow).then_inc(rstd_ready, 1)
            pool.wait_ge(rstd_ready, m + 1)
            nc.gpsimd.tensor_tensor(shift[:, :], rstd[:, :], neg_mean[:, :], ALU.mult).then_inc(shift_ready, 1)

        def pool_gamma(pool, m, par, between=lambda: None):
            pool.wait_ge(y_normed, m + 1)
            nc.gpsimd.tensor_tensor(y[par][:, :, :], y[par][:, :, :],
                                    gamma_sb[:, :].unsqueeze(1).to_broadcast([P, TILES, D]),
                                    ALU.mult).then_inc(y_gamma, 1)
            between()
            pool.wait_ge(y_gamma, m + 1)
            nc.gpsimd.tensor_tensor(y[par][:, :, :], y[par][:, :, :],
                                    beta_sb[:, :].unsqueeze(1).to_broadcast([P, TILES, D]),
                                    ALU.add).then_inc(y_beta, 1)

        @block.gpsimd
        def _(pool):
            pool.memset(ident[:, :], 0.0).then_inc(s_ident, 1)
            pool.wait_ge(s_ident, 1)
            pool.affine_select(out=ident[:, :], in_=ident[:, :], compare_op=ALU.not_equal, fill=1.0,
                               base=0, pattern=[[-1, P]], channel_multiplier=1).then_inc(s_ident, 1)
            pool.wait_ge(s_ident, 2)
            pool.tensor_copy(ident16[:, :], ident[:, :]).then_inc(s_ident, 1)
            pool.memset(minus_half[:, :], -0.5)
            pool.wait_ge(s_x[0], 16)
            pool.wait_ge(not_full_ready, 2)
            pool_xs(pool, 0)
            pool.memset(v_all[:, :, :, :], 0.0).then_inc(s_zero, 1)
            pool.wait_ge(s_zero, 1)
            pool.memset(v_all[0:KEYS, :, :, DK:DK + 1], 1.0).then_inc(v_ones, 1)
            pool.wait_ge(s_x[1], 16)
            pool.wait_ge(not_full_ready, 4)
            pool_xs(pool, 1)
            mask_product(nc.gpsimd, pool, 2)
            pool.wait_ge(mask16_ready, 3)
            for s in range(PAIRS):
                if s == 4:
                    pool.wait_ge(w_t_done, 4)
                pool.memset(probs[64:P, s, :, :], 0.0).then_inc(s_zero, 1)
            pool.wait_ge(s_zero, 1 + PAIRS)

            def body(b, first, last):
                for h in range(2):
                    n = 2 * b + h
                    if not (first and h == 0):
                        pool_norm(pool, n - 1, 2)
                        pool_norm(pool, n - 1, 3)
                    if first and h == 1:
                        pool.wait_ge(s_gb, 32)
                    if not first:
                        pool_rstd(pool, n - 2)
                    pool_norm(pool, n, 0)
                    pool_norm(pool, n, 1)
                    if not first and not (last and h == 1):
                        pool_gamma(pool, n - 2, h)

            batches(pool, body)
            n = BLOCKS
            pool_norm(pool, n - 1, 2)
            pool_norm(pool, n - 1, 3)
            pool_gamma(pool, n - 3, 1, lambda: pool_rstd(pool, n - 2))
            pool_gamma(pool, n - 2, 0, lambda: pool_rstd(pool, n - 1))


        def act_x_t(act, m, t, bank):
            act.wait_ge(x_t_done, HALVES * m + t + 1)
            if not (isinstance(m, int) and m == 0):
                act.wait_ge(q_done, HALVES * m)
            nc.scalar.activation(x_t[:, t, :], bank[:, :], ACT.Copy).then_inc(x_t_ready, 1)

        def act_q_high(act, m, e, bank):
            act.wait_ge(q_done, HALVES * m + e + 1)
            if not (isinstance(m, int) and m == 0):
                act.wait_ge(s_q_out[e], 32 * m)
            nc.scalar.activation(q16[:, e, 0, :], bank[:, :], ACT.Copy).then_inc(q_high, 1)

        def act_nm(act, m, par):
            act.wait_ge(nm_done, m + 1)
            if not (isinstance(m, int) and m == 0):
                act.wait_ge(s_nm, 16 * m)
            nc.scalar.activation(neg_max_t[:, :], max16[0][0:HEADS, 0:BLOCK], ACT.Copy).then_inc(nm_ready, 1)
            act.wait_ge(nm_ready, m + 1)
            if not (isinstance(m, int) and m < 2):
                act.wait_ge(scores_done, PAIRS * (m - 1))
            act.dma_start(R[par][MAX_ROW:KROWS, :, :], neg_max_t[:, :]).then_inc(s_nm, 16)

        def act_xs(act, m):
            for t in range(TILES):
                nc.scalar.activation(xs[:, t, :], x_all[:, bass.ds(m * TILES + t, 1), :].rearrange("p t d -> p (t d)"),
                                     ACT.Copy, scale=not_full[:, bass.ds(m * TILES + t, 1)]).then_inc(xs_ready, 1)

        def act_apply(act, m, par, half):
            if half == 0:
                act.wait_ge(shift_ready, m + 1)
            for t in range(2 * half, 2 * half + 2):
                last = nc.scalar.activation(y[par][:, t, :], y[par][:, t, :], ACT.Identity,
                                            bias=shift[:, t:t + 1], scale=rstd[:, t:t + 1])
            if half == 1:
                last.then_inc(y_normed, 1)

        @block.scalar
        def _(act):
            def copy_weight(i, count, bank):
                act.wait_ge(w_t_done, count)
                nc.scalar.activation(w_t[i][:, :, :], bank, ACT.Copy).then_inc(w_t_ready, 1)

            def copy_mask(i, bank):
                lo, hi = MASK_TURNS[i]
                act.wait_ge(mask_t_done, i + 1)
                nc.scalar.activation(mask_t[:, lo:hi, :], bank[0:KEYS, 0:(hi - lo) * BLOCK].rearrange("k (m q) -> k m q", q=BLOCK),
                                     ACT.Copy).then_inc(mask_t_ready, 1)

            copy_weight(1, 1, scores_ps[0][:, 0, :])
            for e in range(HALVES):
                act.wait_ge(k_done, e + 1)
                nc.scalar.activation(k16[:, 0, e, :], max_ps[e][:, 0:BATCH * KEYS], ACT.Copy,
                                     scale=KSCALE).then_inc(k_high, 1)
            copy_weight(0, 2, scores_ps[0][:, 1, :])
            copy_mask(0, work16)
            for t in range(HALVES):
                act_x_t(act, 0, t, scores_ps[t][:, 0, :])
            for e in range(HALVES):
                act_q_high(act, 0, e, (pv_ps, work_ps)[e])
            copy_weight(2, 3, max_ps[0][:, :])
            for t in range(HALVES):
                act_x_t(act, 1, t, scores_ps[1][:, t, :])
            act.wait_ge(s_kb, 16 * 3)
            act.wait_ge(s_tail, 32)
            nc.scalar.activation(kb_max[0:QROWS, :, :], kb_all[:, :, 0:KEYS], ACT.Copy).then_inc(kb_max_ready, 1)
            for e in range(HALVES):
                act_q_high(act, 1, e, scores_ps[0][:, e, :])
            copy_mask(1, pv16)
            nc.scalar.activation(kb_scores[0:QROWS, :, :], kb_all[:, :, 0:KEYS], ACT.Copy).then_inc(kb_scores_ready, 1)
            copy_weight(3, 4, scores_ps[1][:, 1, :])
            for i, bank in ((2, pv16), (3, work16), (4, scores16)):
                copy_mask(i, bank)
            act_nm(act, 0, 0)
            for i in range(2):
                act.wait_ge(v_done, i + 1)
                act.wait_ge(v_ones, 1)
                nc.scalar.activation(v_all[0:KEYS, 2 * i:2 * i + 2, :, 0:DK],
                                     (pv_ps, work_ps)[i][0:KEYS, :].rearrange("k (b h d) -> k b h d", b=2, d=DK),
                                     ACT.Copy).then_inc(v_ready, 1)

            def body(b, first, last):
                for h in range(2):
                    n = 2 * b + h
                    if first:
                        act.wait_ge(s_x[n + 2], 16)
                    if not last:
                        act_xs(act, n + 2)
                    for s in range(STEPS):
                        act.wait_ge(scores_done, PAIRS * n + s + 1)
                        if not (first and h == 0):
                            act.wait_ge(pv_done, 4 * (n - 1) + 2 * (s // 4) + 2)
                        nc.scalar.activation(probs[0:KEYS, s, :, :], scores_ps[s % 2][0:KEYS, :, :],
                                             ACT.Exp).then_inc(exp_done, 1)
                        if not last:
                            if s in XT_AT:
                                act_x_t(act, n + 2, XT_AT.index(s), work_ps)
                            if s in Q_AT:
                                act_q_high(act, n + 2, Q_AT.index(s), work_ps)
                        if s == NM_AT and not (last and h == 1):
                            act_nm(act, n + 1, 1 - h)
                        if s in APPLY_AT and not first:
                            act_apply(act, n - 2, h, APPLY_AT.index(s))
                if first:
                    for m in range(4, BLOCKS):
                        act.wait_ge(s_x[m], 16)

            batches(act, body)
            for half in range(2):
                act_apply(act, BLOCKS - 2, 0, half)


        def dve_mask(dve, part):
            n, (t0, t1) = part + 1, (i * TILES for i in MASK_PARTS[part])
            dve.wait_ge(s_mask[min(part, 1)], 16)
            nc.vector.tensor_scalar(mask_eq[:, t0:t1, :], mask_all[:, t0:t1, :], 1.0, None, ALU.is_equal).then_inc(eq_ready, 1)
            dve.wait_ge(eq_ready, n)
            nc.vector.tensor_reduce(all_masked[:, t0:t1], mask_eq[:, t0:t1, :], AX.X, ALU.min).then_inc(full_ready, 1)
            dve.wait_ge(full_ready, n)
            nc.vector.tensor_scalar(not_full[:, t0:t1], all_masked[:, t0:t1], -1.0, 1.0, ALU.mult, ALU.add).then_inc(not_full_ready, 1)
            nc.vector.tensor_scalar(not_full_big[:, t0:t1], all_masked[:, t0:t1], -BIG, BIG, ALU.mult, ALU.add).then_inc(not_full_ready, 1)

        def dve_q_low(dve, m, e, bank):
            dve.wait_ge(q_high, HALVES * m + e + 1)
            nc.vector.tensor_tensor(q16[:, e, 1, :], bank[:, :], q16[:, e, 0, :], ALU.subtract).then_inc(q_low, 1)

        def dve_max(dve, m, u):
            (lo, hi), t = GROUPS[u // TILES], u % TILES
            dve.wait_ge(max_done, UNITS * m + u + 1)
            if u == 0 and not (isinstance(m, int) and m == 0):
                dve.wait_ge(nm_done, m)
            nc.vector.tensor_reduce(neg_max[:, t, lo:hi],
                                    max_ps[u % 2][:, 0:(hi - lo) * KEYS].rearrange("p (h k) -> p h k", k=KEYS),
                                    AX.X, ALU.max, negate=True).then_inc(max_reduced, 1)

        def dve_turn(dve, m, t, bank):
            dve.wait_ge(pv_done, 4 * m + t + 1)
            if not (isinstance(m, int) and m == 0 and t < 2):
                dve.wait_ge(ctx_normed, 4 * m + t - 1)
            nc.vector.transpose(ctx_q[:, t % 2, :, :], bank[:, :]).then_inc(pv_turned, 1)
            dve.wait_ge(pv_turned, 4 * m + t + 1)
            nc.vector.reciprocal(rden[:, t % 2, :], ctx_q[:, t % 2, :, DK]).then_inc(rden_ready, 1)

        def dve_ctx_e(dve, m, v, par):
            dve.wait_ge(ctx_normed, 4 * m + 2 * v + 2)
            if not (isinstance(m, int) and m < 2):
                dve.wait_ge(out_done, 2 * (m - 1))
            nc.vector.transpose(ctx_e[par][:, v, :], ctx_n[:, v, :, :]).then_inc(ctx_e_ready, 1)

        def dve_residual(dve, m, rows, stores, half, bank):
            dve.wait_ge(out_done, 2 * m + half + 1)
            if stores is not None:
                dve.wait_ge(*stores)
            nc.vector.tensor_tensor(rows[:, 2 * half:2 * half + 2, :], bank[:, :].rearrange("p (t d) -> p t d", d=D),
                                    x_all[:, bass.ds(m * TILES + 2 * half, 2), :], ALU.add).then_inc(out_ready, 1)

        def dve_stats(dve, m, rows, t):
            if t > 0:
                dve.wait_ge(bn_ready, TILES * m + t)
            if t % 2 == 0:
                dve.wait_ge(out_ready, 2 * m + t // 2 + 1)
            nc.vector.bn_stats(bn[:, t, :], rows[:, t, :]).then_inc(bn_ready, 1)
            if t > 0:
                nc.vector.bn_aggr(mean_var[:, t - 1, :], bn[:, t - 1, :]).then_inc(mv_ready, 1)

        def dve_variance(dve, m):
            if not (isinstance(m, int) and m == 0):
                dve.wait_ge(shift_ready, m)
            dve.wait_ge(bn_ready, TILES * (m + 1))
            dve.wait_ge(mv_ready, TILES * (m + 1) - 1)
            nc.vector.tensor_scalar(var_eps[:, 0:TILES - 1], mean_var[:, 0:TILES - 1, 1], EPS, None, ALU.add).then_inc(ve_ready, 1)
            nc.vector.bn_aggr(mean_var[:, TILES - 1, :], bn[:, TILES - 1, :]).then_inc(mv_ready, 1)
            dve.wait_ge(mv_ready, TILES * (m + 1))
            nc.vector.tensor_scalar(var_eps[:, TILES - 1:TILES], mean_var[:, TILES - 1:TILES, 1], EPS, None, ALU.add).then_inc(ve_ready, 1)
            nc.vector.tensor_scalar(neg_mean[:, :], mean_var[:, :, 0], -1.0, None, ALU.mult).then_inc(ve_ready, 1)

        @block.vector
        def _(dve):
            nc.vector.memset(kb_tail[:, :, :], 1.0).then_inc(tail_ready, 1)
            dve.wait_ge(s_ident, 3)
            dve.wait_ge(tail_ready, 1)
            nc.vector.tensor_scalar(kb_tail[0:KEYS, 0, :], ident[0:KEYS, 0:KEYS], -BIG, None, ALU.mult).then_inc(tail_ready, 1)
            dve.wait_ge(tail_ready, 2)
            nc.vector.tensor_copy(kb_tail[0:KEYS, 1:HEADS, :],
                                  kb_tail[0:KEYS, 0, :].unsqueeze(1).to_broadcast([KEYS, HEADS - 1, KEYS])
                                  ).then_inc(tail_ready, 1)
            dve_mask(dve, 0)
            mask_product(nc.vector, dve, 0)
            for t in range(HALVES):
                dve.wait_ge(c_t_done, t + 1)
                nc.vector.tensor_copy(ctx_t[:, t, :], scores_ps[1][:, t, 0:BATCH * KEYS]).then_inc(c_t_ready, 1)
            for e in range(HALVES):
                dve.wait_ge(k_high, e + 1)
                nc.vector.scalar_tensor_tensor(out=k16[:, 1, e, :], in0=max_ps[e][:, 0:BATCH * KEYS],
                                               scalar=KSCALE, in1=k16[:, 0, e, :],
                                               op0=ALU.mult, op1=ALU.subtract).then_inc(k_low, 1)
            dve_mask(dve, 1)
            mask_product(nc.vector, dve, 1)
            for e in range(HALVES):
                dve_q_low(dve, 0, e, (pv_ps, work_ps)[e])
            dve_mask(dve, 2)
            for u in range(UNITS):
                dve_max(dve, 0, u)
                if u < HALVES:
                    dve_q_low(dve, 1, u, scores_ps[0][:, u, :])

            def body(b, first, last):
                for h in range(2):
                    n = 2 * b + h
                    for s in range(STEPS):
                        if s == Q_AT[0] + 1 and not last:
                            dve_q_low(dve, n + 2, 0, work_ps)
                        if not (last and h == 1):
                            for u in range(UNITS_AT[s]):
                                dve_max(dve, n + 1, UNIT_START[s] + u)
                        if s == Q_AT[1] + 1 and not last:
                            dve_q_low(dve, n + 2, 1, work_ps)
                        if s in PV_AT[0:2] and not (first and h == 0):
                            dve_turn(dve, n - 1, 2 + PV_AT.index(s), pv_ps)
                        if s in PV_AT[2:4]:
                            dve_turn(dve, n, PV_AT.index(s) - 2, pv_ps)
                        if s == 6 and h == 0 and not last:
                            nc.vector.tensor_copy(kb_max[0:QROWS, :, :], kb_all[:, :, bass.ds((b + 1) * KEYS, KEYS)]
                                                  ).then_inc(kb_max_ready, 1)
                        if s == 7 and h == 1 and not last:
                            nc.vector.tensor_copy(kb_scores[0:QROWS, :, :], kb_all[:, :, bass.ds((b + 1) * KEYS, KEYS)]
                                                  ).then_inc(kb_scores_ready, 1)
                        if s in OUT_AT and not (first and h == 0):
                            stored = b - 1 if h == 0 else b
                            dve_residual(dve, n - 1, y[1 - h],
                                         None if isinstance(stored, int) and stored == 0 else (s_store[1 - h], 16 * stored),
                                         OUT_AT.index(s), work_ps)
                        if s in STATS_AT and not first:
                            dve_stats(dve, n - 2, y[h], STATS_AT.index(s))
                        if s in CTX_AT and not (first and h == 0):
                            dve_ctx_e(dve, n - 1, CTX_AT.index(s), 1 - h)
                        if s == VARIANCE_AT and not first:
                            dve_variance(dve, n - 2)
                        if s == 3 and h == 0:
                            if not first:
                                dve.wait_ge(pv_done, 4 * n)
                            else:
                                dve.wait_ge(v_ready, 2)
                            nc.vector.tensor_copy(v_now[:, :, :], v_all[:, bass.ds(b, 1), :, :].rearrange("p a h k -> p (a h) k")
                                                  ).then_inc(v_now_ready, 1)
            batches(dve, body)
            n = BLOCKS
            dve_ctx_e(dve, n - 1, 0, 1)
            dve_turn(dve, n - 1, 2, pv_ps)
            dve_turn(dve, n - 1, 3, max_ps[0])
            dve_ctx_e(dve, n - 1, 1, 1)
            for t in range(TILES):
                dve_stats(dve, n - 2, y[0], t)
            dve_variance(dve, n - 2)
            for half in range(2):
                dve_residual(dve, n - 1, xs, None, half, (work_ps, max_ps[1])[half])
                if half == 0:
                    for t in range(2):
                        dve_stats(dve, n - 1, xs, t)
            for t in range(2, TILES):
                dve_stats(dve, n - 1, xs, t)
            dve_variance(dve, n - 1)
            dve.wait_ge(s_gb, 32)
            dve.wait_ge(ve_ready, 3 * n)
            for t in range(TILES):
                last = nc.vector.scalar_tensor_tensor(out=xs[:, t, :], in0=xs[:, t, :], scalar=neg_mean[:, t:t + 1],
                                                      in1=gamma_sb[:, :], op0=ALU.add, op1=ALU.mult)
            last.then_inc(y_last, 1)
            dve.wait_ge(y_last, 1)
            dve.wait_ge(rstd_ready, n)
            for half in range(2):
                for t in range(2 * half, 2 * half + 2):
                    last = nc.vector.scalar_tensor_tensor(out=xs[:, t, :], in0=xs[:, t, :], scalar=rstd[:, t:t + 1],
                                                          in1=beta_sb[:, :], op0=ALU.mult, op1=ALU.add)
                last.then_inc(y_last, 1)

        def pe_scores(pe, m, s, par, b):
            if s == 0:
                pe.wait_ge(kb_scores_ready, b + 1)
                pe.wait_ge(s_nm, 16 * (m + 1))
            if not (isinstance(m, int) and m == 0 and s < 2):
                pe.wait_ge(exp_done, PAIRS * m + s - 1)
            for i in range(2):
                last = nc.tensor.matmul(scores_ps[s % 2][0:KEYS, i, :], kb_scores[:, 2 * s + i, :], R[par][:, 2 * s + i, :],
                                        start=True, stop=True)
            last.then_inc(scores_done, 1)

        def pe_max(pe, m, u, par, b):
            (lo, hi), t = GROUPS[u // TILES], u % TILES
            if u == 0:
                pe.wait_ge(kb_max_ready, b + 1)
            if t == 0:
                pe.wait_ge(s_R[par][u // TILES], 16 * RLOADS * (b + 1))
            if not (isinstance(m, int) and m == 0 and u < 2):
                pe.wait_ge(max_reduced, UNITS * m + u - 1)
            if u == 0 and not (isinstance(m, int) and m == 0):
                pe.wait_ge(nm_ready, m)
            for i in range(hi - lo):
                last = nc.tensor.matmul(max_ps[u % 2][:, i * KEYS:(i + 1) * KEYS],
                                        R[par][0:MAX_ROW, lo + i, t * P:(t + 1) * P], kb_max[0:MAX_ROW, lo + i, :],
                                        start=True, stop=True)
            last.then_inc(max_done, 1)

        def pe_nm(pe, m):
            pe.wait_ge(max_reduced, UNITS * (m + 1))
            for t in range(TILES):
                last = nc.tensor.transpose(max16[0][0:HEADS, t * P:(t + 1) * P], neg_max[:, t, :], ident16[:, :])
            last.then_inc(nm_done, 1)

        def pe_pv(pe, m, t, batches_ready, bank):
            v, u = t // 2, t % 2
            if t == 0:
                pe.wait_ge(v_now_ready, batches_ready)
            pe.wait_ge(exp_done, PAIRS * m + 4 * (v + 1))
            if bank is pv_ps and not (isinstance(m, int) and m == 0 and t == 0):
                pe.wait_ge(pv_turned, 4 * m + t)
            for j in range(4):
                last = nc.tensor.matmul(bank[32 * j:32 * (j + 1), :], v_now[:, 8 * v + 2 * j + u, :],
                                        probs[:, 4 * v + j, u, :], start=True, stop=True)
            last.then_inc(pv_done, 1)

        def pe_mask_t(pe, lo, hi, bank):
            for t in range(lo * TILES, hi * TILES):
                c = (t - lo * TILES) * P
                last = nc.tensor.transpose(bank[0:KEYS, c:c + P], mask16[:, t, :], ident16[:, :])
            last.then_inc(mask_t_done, 1)

        def pe_x_t(pe, m, d, bank):
            if d == 0:
                pe.wait_ge(xs_ready, TILES * (m + 1))
            for t in range(TILES):
                last = nc.tensor.transpose(bank[:, t * P:(t + 1) * P], xs[:, t, d * P:(d + 1) * P], ident[:, :])
            last.then_inc(x_t_done, 1)

        def pe_q(pe, m, e, bank):
            pe.wait_ge(x_t_ready, HALVES * (m + 1))
            for t in range(HALVES):
                last = nc.tensor.matmul(bank[:, :], w_t[0][:, t, e * P:(e + 1) * P], x_t[:, t, :],
                                        start=(t == 0), stop=(t == HALVES - 1))
            last.then_inc(q_done, 1)

        def pe_out(pe, m, par, half, bank):
            if half == 0:
                pe.wait_ge(ctx_e_ready, HALVES * (m + 1))
            for i in range(2):
                q0 = (2 * half + i) * P
                for v in range(HALVES):
                    last = nc.tensor.matmul(bank[:, i * D:(i + 1) * D], ctx_e[par][:, v, q0:q0 + P], w_t[3][:, v, :],
                                            start=(v == 0), stop=(v == HALVES - 1))
            last.then_inc(out_done, 1)

        @block.tensor
        def _(pe):
            def turn_weight(i, bank):
                pe.wait_ge(s_w[i], 16)
                for t in range(HALVES):
                    for e in range(HALVES):
                        last = nc.tensor.transpose(bank[:, t * D + e * P:t * D + (e + 1) * P],
                                                   w_in[i][:, e, t * P:(t + 1) * P], ident[:, :])
                last.then_inc(w_t_done, 1)

            pe.wait_ge(s_ident, 3)
            turn_weight(1, scores_ps[0][:, 0, :])
            pe.wait_ge(s_ctx, 16)
            for t in range(HALVES):
                for b in range(BATCH):
                    last = nc.tensor.transpose(scores_ps[1][:, t, b * KEYS:(b + 1) * KEYS], ctx_sb[:, b, t * P:(t + 1) * P],
                                               ident[0:KEYS, 0:KEYS])
                last.then_inc(c_t_done, 1)
            pe.wait_ge(c_t_ready, HALVES)
            pe.wait_ge(w_t_ready, 1)
            for e in range(HALVES):
                for t in range(HALVES):
                    last = nc.tensor.matmul(max_ps[e][:, 0:BATCH * KEYS], w_t[1][:, t, e * P:(e + 1) * P],
                                            ctx_t[:, t, :], start=(t == 0), stop=(t == HALVES - 1))
                last.then_inc(k_done, 1)
            turn_weight(0, scores_ps[0][:, 1, :])
            pe.wait_ge(mask16_ready, 1)
            pe_mask_t(pe, *MASK_TURNS[0], work16)
            for t in range(HALVES):
                pe_x_t(pe, 0, t, scores_ps[t][:, 0, :])
            pe.wait_ge(w_t_ready, 2)
            pe.wait_ge(mask_t_ready, 1)
            for e in range(HALVES):
                pe_q(pe, 0, e, (pv_ps, work_ps)[e])
            pe.wait_ge(k_low, HALVES)
            turn_weight(2, max_ps[0][:, :])
            for t in range(HALVES):
                pe_x_t(pe, 1, t, scores_ps[1][:, t, :])
            for e in range(HALVES):
                pe_q(pe, 1, e, scores_ps[0][:, e, :])
            pe.wait_ge(q_low, HALVES)
            pe.wait_ge(mask16_ready, 2)
            pe_mask_t(pe, *MASK_TURNS[1], pv16)
            pe.wait_ge(w_t_ready, 3)
            for u in range(UNITS):
                pe_max(pe, 0, u, 0, 0)
                if u == 5:
                    pe.wait_ge(x_t_ready, 2 * HALVES)
                    turn_weight(3, scores_ps[1][:, 1, :])
                if u == 7:
                    pe.wait_ge(mask16_ready, 3)
                    pe.wait_ge(mask_t_ready, 2)
                if u in (7, 8, 9):
                    pe_mask_t(pe, *MASK_TURNS[u - 5], (pv16, work16, scores16)[u - 7])
            pe_nm(pe, 0)
            pe.wait_ge(mask_t_ready, len(MASK_TURNS))
            for b in range(BATCH):
                for t in range(HALVES):
                    last = nc.tensor.matmul((pv_ps, work_ps)[b // 2][0:KEYS, (b % 2) * D:(b % 2 + 1) * D],
                                            ctx_t[:, t, b * KEYS:(b + 1) * KEYS],
                                            w_t[2][:, t, :], start=(t == 0), stop=(t == HALVES - 1))
                if b % 2 == 1:
                    last.then_inc(v_done, 1)
            pe.wait_ge(q_low, 2 * HALVES)
            pe.wait_ge(s_zero, 1 + PAIRS)

            def body(b, first, last):
                for h in range(2):
                    n = 2 * b + h
                    for s in range(STEPS):
                        pe_scores(pe, n, s, h, b)
                        if not (last and h == 1):
                            for u in range(UNITS_AT[s]):
                                pe_max(pe, n + 1, UNIT_START[s] + u, 1 - h, b + h)
                        if s in PV_AT[0:2] and not (first and h == 0):
                            pe_pv(pe, n - 1, 2 + PV_AT.index(s), b, pv_ps)
                        if s in PV_AT[2:4]:
                            pe_pv(pe, n, PV_AT.index(s) - 2, b + 1, pv_ps)
                        if s == NM_AT and not (last and h == 1):
                            pe_nm(pe, n + 1)
                        if not last:
                            if s == XT_AT[0]:
                                if first and h == 0:
                                    pe.wait_ge(v_ready, 2)
                                else:
                                    pe.wait_ge(out_ready, 2 * (n - 1))
                                pe_x_t(pe, n + 2, 0, work_ps)
                            if s == XT_AT[1]:
                                pe.wait_ge(x_t_ready, HALVES * (n + 2) + 1)
                                pe_x_t(pe, n + 2, 1, work_ps)
                            if s == Q_AT[0]:
                                pe_q(pe, n + 2, 0, work_ps)
                            if s == Q_AT[1]:
                                pe.wait_ge(q_low, HALVES * (n + 2) + 1)
                                pe_q(pe, n + 2, 1, work_ps)
                        if s == OUT_AT[0] and not (first and h == 0):
                            if not last:
                                pe.wait_ge(q_low, HALVES * (n + 3))
                            else:
                                pe.wait_ge(out_ready, 2 * (n - 1))
                            pe_out(pe, n - 1, 1 - h, 0, work_ps)
                        if s == OUT_AT[1] and not (first and h == 0):
                            pe.wait_ge(out_ready, 2 * (n - 1) + 1)
                            pe_out(pe, n - 1, 1 - h, 1, work_ps)

            batches(pe, body)
            n = BLOCKS
            pe_pv(pe, n - 1, 2, BATCH, pv_ps)
            pe_pv(pe, n - 1, 3, BATCH, max_ps[0])
            pe.wait_ge(out_ready, 2 * (n - 1))
            for half in range(2):
                pe_out(pe, n - 1, 1, half, (work_ps, max_ps[1])[half])


_INS = ['x', 'ctx_1024', 'mask_BxSxS2_ik1', 'L0_xattn_W_Q', 'L0_xattn_W_K', 'L0_xattn_W_V', 'L0_xattn_W_O',
        'L0_xattn_gamma', 'L0_xattn_beta']


def kernel(**inputs):
    import numpy as np
    import concourse.bacc as bacc
    from concourse.bass_utils import run_bass_kernel_spmd

    nc = bacc.Bacc("TRN2", target_bir_lowering=False, num_devices=1)
    arrays, args = {}, []
    for name in _INS:
        a = np.ascontiguousarray(inputs[name])
        arrays[f"in_{name}"] = a
        args.append(nc.dram_tensor(f"in_{name}", a.shape, mybir.dt.from_np(a.dtype), kind="ExternalInput").ap())
    out = nc.dram_tensor("out", (BATCH, SEQ, D), F32, kind="ExternalOutput").ap()
    cross_attention(nc, *args, out)
    return run_bass_kernel_spmd(nc, [arrays], core_ids=[0]).results[0]["out"]
```

```python
from contextlib import ExitStack

import concourse.bass as bass
from concourse import mybir

F32 = mybir.dt.float32
F16 = mybir.dt.float16
I32 = mybir.dt.int32
ALU = mybir.AluOpType
ACT = mybir.ActivationFunctionType
AX = mybir.AxisListType

P = 128
BATCH = 4
SEQ = 1024
D = 256
HEADS = 16
DK = D // HEADS
KEYS = 77
EPS = 1e-5
BLOCK = 512
BLOCKS = BATCH * SEQ // BLOCK
TILES = BLOCK // P
HALVES = D // P
PAIRS = HEADS // 2
STEPS = PAIRS
QROWS = 3 * DK
MASK_ROW = QROWS
MAX_ROW = MASK_ROW + KEYS
KROWS = MAX_ROW + 1
BIG = 32768.0
GROUPS = [(0, 6), (6, 12), (12, 16)]
UNITS = len(GROUPS) * TILES
UNITS_AT = [2, 2, 2, 2, 2, 2, 0, 0]
UNIT_START = [sum(UNITS_AT[:s]) for s in range(STEPS)]
PV_AT = (0, 3, 5, 7)
NM_AT = 5
XT_AT = (0, 1)
Q_AT = (2, 3)
OUT_AT = (6, 7)
STATS_AT = (0, 1, 2, 3)
VARIANCE_AT = 5
APPLY_AT = (6, 7)
CTX_AT = (1, 5)
LAST_VARIANCE_AT = 4
LAST_APPLY_AT = (5, 6)
POOL_TILES = TILES - 1
RLOADS = 3
GROUPS_OF = [[g for g, (lo, hi) in enumerate(GROUPS) if lo < (e + 1) * PAIRS and hi > e * PAIRS] for e in range(HALVES)]
MASK_PARTS = [(0, 1), (1, 2), (2, 4), (4, BLOCKS)]
MASK_LOADS = [(0, 1), (1, 4), (4, BLOCKS)]
MASK_TURNS = [(0, 1), (1, 2), (2, 4), (4, 6), (6, BLOCKS)]
WO_U, MASK_U = 5, 7
KSCALE = 1.0 / float(DK) ** 0.5


def cross_attention(nc, x, ctx_in, mask, w_q, w_k, w_v, w_o, gamma, beta, out):
    stack = ExitStack()
    with stack:
        def sb(name, shape, dt=F32):
            return stack.enter_context(nc.sbuf_tensor(name, shape, dt))

        def ps(name, shape, dt=F32):
            return stack.enter_context(nc.psum_tensor(name, shape, dt))

        def sem(name):
            return stack.enter_context(nc.semaphore(name))

        q_scratch = [nc.dram_tensor(f"q_scratch{i}", [HEADS, 2, DK, BLOCK], F16, kind="Internal").ap() for i in range(2)]
        k_scratch = nc.dram_tensor("k_scratch", [2, HEADS, DK, BATCH * KEYS], F16, kind="Internal").ap()

        x_all = sb("x_all", [P, BLOCKS * TILES, D])
        mask_all = sb("mask_all", [P, BLOCKS * TILES, KEYS], I32)
        w_t = [sb(f"w_t{i}", [P, HALVES, D]) for i in range(4)]
        ctx_sb = sb("ctx_sb", [KEYS, BATCH, D])
        ctx_t = sb("ctx_t", [P, HALVES, BATCH * KEYS])
        k16 = sb("k16", [P, 2, HALVES, BATCH * KEYS], F16)
        kb_all = sb("kb_all", [QROWS, HEADS, BATCH * KEYS], F16)
        kb_scores = sb("kb_scores", [KROWS, HEADS, KEYS], F16)
        kb_max = sb("kb_max", [KROWS, HEADS, KEYS], F16)
        kb_tail = sb("kb_tail", [KEYS + 1, HEADS, KEYS], F16)
        v_all = sb("v_all", [P, BATCH, HEADS, 32])
        v_now = sb("v_now", [P, HEADS, 32])
        ident = sb("ident", [P, P])
        ident16 = sb("ident16", [P, P], F16)
        gamma_sb = sb("gamma_sb", [P, D])
        beta_sb = sb("beta_sb", [P, D])
        minus_half = sb("minus_half", [P, TILES])
        all_masked = sb("all_masked", [P, BLOCKS * TILES])
        not_full = sb("not_full", [P, BLOCKS * TILES])
        not_full_big = sb("not_full_big", [P, BLOCKS * TILES])
        mask16 = sb("mask16", [P, BLOCKS * TILES, KEYS], F16)
        mask_t = sb("mask_t", [KEYS, BLOCKS, BLOCK], F16)
        xs = sb("xs", [P, TILES, D])
        x_t = sb("x_t", [P, HALVES, BLOCK])
        q16 = sb("q16", [P, HALVES, 2, BLOCK], F16)
        R = [sb(f"R{i}", [KROWS, HEADS, BLOCK], F16) for i in range(2)]
        neg_max = sb("neg_max", [P, TILES, HEADS], F16)
        neg_max_t = sb("neg_max_t", [HEADS, BLOCK], F16)
        probs = sb("probs", [P, PAIRS, 2, BLOCK])
        y = [sb(f"y{i}", [P, TILES, D]) for i in range(2)]
        spare = probs[:, 4:6, :, :].rearrange("p s i q -> p (s i q)").rearrange("p (i t d) -> p i t d", t=HALVES, d=D)
        w_in = [spare[:, i, :, :] for i in range(3)] + [y[1][:, 0:HALVES, :]]
        mask_eq = probs[:, 6:8, :, :].rearrange("p s i q -> p (s i q)").bitcast(F16)[:, 0:BLOCKS * TILES * KEYS].rearrange(
            "p (t k) -> p t k", k=KEYS)
        ctx_q = sb("ctx_q", [P, 2, BLOCK // 32, 32])
        rden = sb("rden", [P, 2, BLOCK // 32])
        ctx_n = sb("ctx_n", [P, HALVES, BLOCK // 32, 32])
        ctx_e = [sb(f"ctx_e{i}", [P, HALVES, BLOCK]) for i in range(2)]
        bn = sb("bn", [P, TILES, 6])
        mean_var = sb("mean_var", [P, TILES, 2])
        var_eps = sb("var_eps", [P, TILES])
        neg_mean = sb("neg_mean", [P, TILES])
        rstd = sb("rstd", [P, TILES])
        shift = sb("shift", [P, TILES])

        scores_ps = [ps(f"scores_ps{i}", [P, 2, BLOCK]) for i in range(2)]
        max_ps = [ps(f"max_ps{i}", [P, BLOCK]) for i in range(2)]
        pv_ps = ps("pv_ps", [P, BLOCK])
        work_ps = ps("work_ps", [P, BLOCK])
        work16 = work_ps[:, :].bitcast(F16)
        pv16 = pv_ps[:, :].bitcast(F16)
        max16 = [t[:, :].bitcast(F16) for t in max_ps]

        s_w = [sem(f"s_w{i}") for i in range(3)]
        s_ctx = sem("s_ctx")
        s_gb = sem("s_gb")
        s_x = [sem(f"s_x{i}") for i in range(BLOCKS)]
        s_mask = [sem(f"s_mask{i}") for i in range(len(MASK_LOADS))]
        s_ident = sem("s_ident")
        s_zero = sem("s_zero")
        w_t_done, w_t_ready = sem("w_t_done"), sem("w_t_ready")
        c_t_done, c_t_ready = sem("c_t_done"), sem("c_t_ready")
        k_done, k_high, k_low = sem("k_done"), sem("k_high"), sem("k_low")
        v_done, v_ready, v_ones = sem("v_done"), sem("v_ready"), sem("v_ones")
        s_k_out = sem("s_k_out")
        s_kb = sem("s_kb")
        tail_ready = sem("tail_ready")
        s_tail = [sem("s_tail_max"), sem("s_tail_scores")]
        kb_scores_ready, kb_max_ready, v_now_ready = sem("kb_scores_ready"), sem("kb_max_ready"), sem("v_now_ready")
        eq_ready, full_ready, not_full_ready, mask16_ready = sem("eq_ready"), sem("full_ready"), sem("not_full_ready"), sem("mask16_ready")
        xs_ready = sem("xs_ready")
        mask_t_done, mask_t_ready = sem("mask_t_done"), sem("mask_t_ready")
        x_t_done, x_t_ready = sem("x_t_done"), sem("x_t_ready")
        q_done, q_high, q_low = sem("q_done"), sem("q_high"), sem("q_low")
        s_q_out = [sem(f"s_q_out{e}") for e in range(HALVES)]
        s_R = [[sem(f"s_R{i}_{g}") for g in range(len(GROUPS))] for i in range(2)]
        max_done, max_reduced = sem("max_done"), sem("max_reduced")
        nm_done, nm_ready, s_nm = sem("nm_done"), sem("nm_ready"), sem("s_nm")
        scores_done, exp_done = sem("scores_done"), sem("exp_done")
        pv_done, pv_turned = sem("pv_done"), sem("pv_turned")
        rden_ready, ctx_normed, ctx_e_ready = sem("rden_ready"), sem("ctx_normed"), sem("ctx_e_ready")
        out_done, out_ready = sem("out_done"), sem("out_ready")
        bn_ready, mv_ready, ve_ready, rstd_ready, shift_ready = sem("bn_ready"), sem("mv_ready"), sem("ve_ready"), sem("rstd_ready"), sem("shift_ready")
        y_normed, y_gamma, y_beta = sem("y_normed"), sem("y_gamma"), sem("y_beta")
        y_dve = sem("y_dve")
        y_last = sem("y_last")
        s_y = [sem(f"s_y{i}") for i in range(2)]

        x_rows = x.rearrange("b (m p t) d -> p (b m) t d", p=P, t=TILES)
        mask_rows = mask.rearrange("b (m p t) k -> p (b m) t k", p=P, t=TILES)
        out_rows = out.rearrange("b (m p t) d -> p (b m) t d", p=P, t=TILES)

        block = stack.enter_context(nc.Block())

        def batches(eng, body):
            body(0, True, False)
            with eng.Fori(1, BATCH - 1) as b:
                body(b, False, False)
            body(BATCH - 1, False, True)


        def store_q(sp, m, par, b, e):
            sp.wait_ge(q_low, HALVES * m + e + 1)
            if not isinstance(b, int) or b > 0:
                for g in GROUPS_OF[e]:
                    sp.wait_ge(s_R[par][g], 16 * RLOADS * b)
            for part in range(2):
                sp.dma_start(q_scratch[par][e * PAIRS:(e + 1) * PAIRS, part, :, :], q16[:, e, part, :]).then_inc(s_q_out[e], 16)

        def load_mask(sp, m, par, g):
            lo, hi = GROUPS[g]
            sp.dma_start(R[par][MASK_ROW:MAX_ROW, lo:hi, :],
                         mask_t[:, bass.ds(m, 1), :].to_broadcast([KEYS, hi - lo, BLOCK])).then_inc(s_R[par][g], 16)

        def load_q(sp, par, g):
            lo, hi = GROUPS[g]
            sp.dma_start(R[par][0:2 * DK, lo:hi, :], q_scratch[par][lo:hi, :, :, :].rearrange("h l d q -> (l d) h q")
                         ).then_inc(s_R[par][g], 16)
            sp.dma_start(R[par][2 * DK:3 * DK, lo:hi, :], q_scratch[par][lo:hi, 0, :, :].rearrange("h d q -> d h q")).then_inc(s_R[par][g], 16)

        def store_out(sp, m, par):
            sp.wait_ge(y_beta, m + 1)
            sp.dma_start(out_rows[:, bass.ds(m, 1), :, :].rearrange("p m t d -> p (m t) d"), y[par][:, :, :]).then_inc(s_y[par], 16)

        @block.sync
        def _(sp):
            def load_weight(i, w):
                sp.dma_start(w_in[i][:, :, :], w.rearrange("(t p) d -> p t d", p=P)).then_inc(s_w[i] if i < 3 else s_y[1], 16)

            def load_masks(i):
                lo, hi = MASK_LOADS[i]
                sp.dma_start(mask_all[:, lo * TILES:hi * TILES, :].rearrange("p (m t) k -> p m t k", t=TILES),
                             mask_rows[:, lo:hi, :, :]).then_inc(s_mask[i], 16)

            def load_x(m):
                sp.dma_start(x_all[:, m * TILES:(m + 1) * TILES, :],
                             x_rows[:, m, :, :]).then_inc(s_x[m], 16)

            load_weight(1, w_k)
            sp.dma_start(ctx_sb[:, :, :], ctx_in.rearrange("b k d -> k b d")).then_inc(s_ctx, 16)
            load_masks(0)
            load_x(0)
            load_weight(0, w_q)
            sp.wait_ge(tail_ready, 3)
            sp.dma_start(kb_max[MASK_ROW:KROWS, :, :], kb_tail[:, :, :]).then_inc(s_tail[0], 16)
            load_weight(2, w_v)
            load_x(1)
            load_masks(1)
            load_weight(3, w_o)
            sp.wait_ge(mask_t_ready, 1)
            for g in range(len(GROUPS)):
                load_mask(sp, 0, 0, g)
            sp.wait_ge(k_low, HALVES)
            sp.dma_start(k_scratch.rearrange("l (e h) d k -> (h d) (l e) k", e=HALVES), k16[:, :, :, :].rearrange("p l e k -> p (l e) k")
                         ).then_inc(s_k_out, 16)
            store_q(sp, 0, 0, 0, 0)
            sp.wait_ge(s_k_out, 16)
            for lo, hi, parts in ((0, 1, k_scratch[0]), (1, 2, k_scratch[0]), (2, 3, k_scratch[1])):
                sp.dma_start(kb_all[lo * DK:hi * DK, :, :], parts.rearrange("h d k -> d h k")).then_inc(s_kb, 16)
            for g in range(len(GROUPS)):
                if g == 0:
                    sp.wait_ge(s_q_out[0], 32)
                if g == 1:
                    store_q(sp, 0, 0, 0, 1)
                    sp.wait_ge(s_q_out[1], 32)
                load_q(sp, 0, g)
            sp.dma_start(kb_scores[MASK_ROW:KROWS, :, :], kb_tail[:, :, :]).then_inc(s_tail[1], 16)
            sp.wait_ge(mask_t_ready, 2)
            load_mask(sp, 1, 1, 0)
            load_masks(2)
            store_q(sp, 1, 1, 0, 0)
            load_mask(sp, 1, 1, 1)
            load_mask(sp, 1, 1, 2)
            load_x(2)
            for g in range(len(GROUPS)):
                if g == 0:
                    sp.wait_ge(s_q_out[0], 64)
                if g == 1:
                    store_q(sp, 1, 1, 0, 1)
                    sp.wait_ge(s_q_out[1], 64)
                load_q(sp, 1, g)
            sp.dma_start(gamma_sb[:, :], gamma.rearrange("(a d) -> a d", a=1).to_broadcast([P, D])).then_inc(s_gb, 16)
            sp.dma_start(beta_sb[:, :], beta.rearrange("(a d) -> a d", a=1).to_broadcast([P, D])).then_inc(s_gb, 16)
            sp.wait_ge(s_nm, 16)
            for m in range(3, 6):
                load_x(m)
            sp.wait_ge(mask_t_ready, 3)

            def body(b, first, last):
                for h in range(2):
                    n = 2 * b + h
                    if first:
                        load_x(6 + h)
                    if not last:
                        store_q(sp, n + 2, h, b + 1, 0)
                        for g in range(len(GROUPS)):
                            sp.wait_ge(scores_done, PAIRS * n + GROUPS[g][1] // 2)
                            load_mask(sp, n + 2, h, g)
                            if g == 0:
                                store_q(sp, n + 2, h, b + 1, 1)
                            for e in range(HALVES):
                                if g == GROUPS_OF[e][0]:
                                    sp.wait_ge(s_q_out[e], 32 * (n + 3))
                            load_q(sp, h, g)
                        if not first:
                            store_out(sp, n - 2, h)
                    else:
                        store_out(sp, n - 2, h)
                if first:
                    sp.wait_ge(mask_t_ready, len(MASK_TURNS))

            batches(sp, body)
            for lo, hi, done, count in ((POOL_TILES, TILES, y_dve, 2), (0, POOL_TILES, y_beta, BLOCKS - 1)):
                sp.wait_ge(done, count)
                sp.dma_start(out_rows[:, BLOCKS - 2, lo:hi, :], y[0][:, lo:hi, :]).then_inc(s_y[0], 16)
            for half in range(2):
                sp.wait_ge(y_last, half + 2)
                sp.dma_start(out_rows[:, BLOCKS - 1, 2 * half:2 * half + 2, :], xs[:, 2 * half:2 * half + 2, :]
                             ).then_inc(s_y[1], 16)
            sp.wait_ge(s_y[0], 16 * (BATCH + 1))
            sp.wait_ge(s_y[1], 16 * (1 + BATCH + 1))


        def mask_product(maths, eng, part):
            t0, t1 = (i * TILES for i in MASK_PARTS[part])
            eng.wait_ge(not_full_ready, 2 * (part + 1))
            maths.tensor_tensor(mask16[:, t0:t1, :], mask_eq[:, t0:t1, :],
                                not_full_big[:, t0:t1].unsqueeze(2).to_broadcast([P, t1 - t0, KEYS]),
                                ALU.mult).then_inc(mask16_ready, 1)

        def pool_xs(pool, m):
            if m > 0:
                pool.wait_ge(x_t_done, HALVES * m)
            nc.gpsimd.tensor_tensor(xs[:, :, :], x_all[:, m * TILES:(m + 1) * TILES, :],
                                    not_full[:, m * TILES:(m + 1) * TILES].unsqueeze(2).to_broadcast([P, TILES, D]),
                                    ALU.mult).then_inc(xs_ready, TILES)

        def pool_norm(pool, m, t):
            v, u = t // 2, t % 2
            pool.wait_ge(rden_ready, 4 * m + t + 1)
            if not (isinstance(m, int) and m == 0):
                pool.wait_ge(ctx_e_ready, 2 * (m - 1) + v + 1)
            nc.gpsimd.tensor_tensor(ctx_n[:, v, :, u * DK:(u + 1) * DK], ctx_q[:, t % 2, :, 0:DK],
                                    rden[:, t % 2, :].unsqueeze(2).to_broadcast([P, BLOCK // 32, DK]),
                                    ALU.mult).then_inc(ctx_normed, 1)

        def pool_rstd(pool, m):
            pool.wait_ge(ve_ready, 3 * (m + 1))
            nc.gpsimd.tensor_tensor(rstd[:, :], var_eps[:, :], minus_half[:, :], ALU.pow).then_inc(rstd_ready, 1)
            pool.wait_ge(rstd_ready, m + 1)
            nc.gpsimd.tensor_tensor(shift[:, :], rstd[:, :], neg_mean[:, :], ALU.mult).then_inc(shift_ready, 1)

        def pool_gamma(pool, m, par, tiles):
            pool.wait_ge(y_normed, m + 1)
            nc.gpsimd.tensor_tensor(y[par][:, 0:tiles, :], y[par][:, 0:tiles, :],
                                    gamma_sb[:, :].unsqueeze(1).to_broadcast([P, tiles, D]),
                                    ALU.mult).then_inc(y_gamma, 1)

        def pool_beta(pool, m, par, tiles):
            pool.wait_ge(y_gamma, m + 1)
            nc.gpsimd.tensor_tensor(y[par][:, 0:tiles, :], y[par][:, 0:tiles, :],
                                    beta_sb[:, :].unsqueeze(1).to_broadcast([P, tiles, D]),
                                    ALU.add).then_inc(y_beta, 1)

        @block.gpsimd
        def _(pool):
            pool.memset(ident[:, :], 0.0).then_inc(s_ident, 1)
            pool.wait_ge(s_ident, 1)
            pool.affine_select(out=ident[:, :], in_=ident[:, :], compare_op=ALU.not_equal, fill=1.0,
                               base=0, pattern=[[-1, P]], channel_multiplier=1).then_inc(s_ident, 1)
            pool.wait_ge(s_ident, 2)
            pool.tensor_copy(ident16[:, :], ident[:, :]).then_inc(s_ident, 1)
            pool.memset(minus_half[:, :], -0.5)
            pool.wait_ge(s_x[0], 16)
            pool.wait_ge(not_full_ready, 2)
            pool_xs(pool, 0)
            pool.memset(v_all[:, :, :, :], 0.0).then_inc(s_zero, 1)
            pool.wait_ge(s_zero, 1)
            pool.memset(v_all[0:KEYS, :, :, DK:DK + 1], 1.0).then_inc(v_ones, 1)
            pool.wait_ge(s_x[1], 16)
            pool.wait_ge(not_full_ready, 4)
            pool_xs(pool, 1)
            mask_product(nc.gpsimd, pool, 2)
            pool.wait_ge(mask16_ready, 3)
            for s in range(PAIRS):
                if s == 4:
                    pool.wait_ge(w_t_done, 3)
                if s == 6:
                    pool.wait_ge(s_zero, 1 + s)
                    pool.wait_ge(s_x[2], 16)
                    pool_xs(pool, 2)
                    mask_product(nc.gpsimd, pool, 3)
                    pool.wait_ge(mask16_ready, 4)
                pool.memset(probs[64:P, s, :, :], 0.0).then_inc(s_zero, 1)
            pool.wait_ge(s_zero, 1 + PAIRS)

            def body(b, first, last):
                for h in range(2):
                    n = 2 * b + h
                    if first and h == 1:
                        pool.wait_ge(s_x[3], 16)
                        pool_xs(pool, 3)
                    if not (first and h == 0):
                        pool_norm(pool, n - 1, 2)
                        pool_norm(pool, n - 1, 3)
                    if first and h == 1:
                        pool.wait_ge(s_gb, 32)
                    if not first:
                        pool_rstd(pool, n - 2)
                    pool_norm(pool, n, 0)
                    if last and h == 1:
                        pool_gamma(pool, n - 2, h, TILES)
                    pool_norm(pool, n, 1)
                    if not first and not (last and h == 1):
                        pool_gamma(pool, n - 2, h, TILES)
                        pool_beta(pool, n - 2, h, TILES)

            batches(pool, body)
            n = BLOCKS
            pool_norm(pool, n - 1, 2)
            pool_norm(pool, n - 1, 3)
            pool_beta(pool, n - 3, 1, TILES)
            pool_rstd(pool, n - 2)
            pool_gamma(pool, n - 2, 0, POOL_TILES)
            pool_rstd(pool, n - 1)
            pool_beta(pool, n - 2, 0, POOL_TILES)


        def act_x_t(act, m, t, bank):
            act.wait_ge(x_t_done, HALVES * m + t + 1)
            if not (isinstance(m, int) and m == 0):
                act.wait_ge(q_done, HALVES * m)
            nc.scalar.activation(x_t[:, t, :], bank[:, :], ACT.Copy).then_inc(x_t_ready, 1)

        def act_q_high(act, m, e, bank):
            act.wait_ge(q_done, HALVES * m + e + 1)
            if not (isinstance(m, int) and m == 0):
                act.wait_ge(s_q_out[e], 32 * m)
            nc.scalar.activation(q16[:, e, 0, :], bank[:, :], ACT.Copy).then_inc(q_high, 1)

        def act_nm(act, m, par):
            act.wait_ge(nm_done, m + 1)
            if not (isinstance(m, int) and m == 0):
                act.wait_ge(s_nm, 16 * m)
            nc.scalar.activation(neg_max_t[:, :], max16[0][0:HEADS, 0:BLOCK], ACT.Copy).then_inc(nm_ready, 1)
            act.wait_ge(nm_ready, m + 1)
            if not (isinstance(m, int) and m < 2):
                act.wait_ge(scores_done, PAIRS * (m - 1))
            act.dma_start(R[par][MAX_ROW:KROWS, :, :], neg_max_t[:, :]).then_inc(s_nm, 16)

        def act_xs(act, m):
            for t in range(TILES):
                nc.scalar.activation(xs[:, t, :], x_all[:, bass.ds(m * TILES + t, 1), :].rearrange("p t d -> p (t d)"),
                                     ACT.Copy, scale=not_full[:, bass.ds(m * TILES + t, 1)]).then_inc(xs_ready, 1)

        def act_apply(act, m, par, half, end=TILES):
            if half == 0:
                act.wait_ge(shift_ready, m + 1)
            for t in range(2 * half, min(2 * half + 2, end)):
                last = nc.scalar.activation(y[par][:, t, :], y[par][:, t, :], ACT.Identity,
                                            bias=shift[:, t:t + 1], scale=rstd[:, t:t + 1])
            if half == 1:
                last.then_inc(y_normed, 1)

        @block.scalar
        def _(act):
            def copy_weight(i, count, bank):
                act.wait_ge(w_t_done, count)
                nc.scalar.activation(w_t[i][:, :, :], bank, ACT.Copy).then_inc(w_t_ready, 1)

            def copy_mask(i, bank):
                lo, hi = MASK_TURNS[i]
                act.wait_ge(mask_t_done, i + 1)
                nc.scalar.activation(mask_t[:, lo:hi, :], bank[0:KEYS, 0:(hi - lo) * BLOCK].rearrange("k (m q) -> k m q", q=BLOCK),
                                     ACT.Copy).then_inc(mask_t_ready, 1)

            copy_weight(1, 1, scores_ps[0][:, 0, :])
            copy_weight(0, 2, scores_ps[0][:, 1, :])
            copy_mask(0, work16)
            for e in range(HALVES):
                act.wait_ge(k_done, e + 1)
                nc.scalar.activation(k16[:, 0, e, :], max_ps[e][:, 0:BATCH * KEYS], ACT.Copy,
                                     scale=KSCALE).then_inc(k_high, 1)
                if e == 0:
                    act_x_t(act, 0, 0, scores_ps[0][:, 0, :])
            for e in range(HALVES):
                act_q_high(act, 0, e, (pv_ps, work_ps)[e])
            copy_weight(2, 3, max_ps[0][:, :])
            for t in range(HALVES):
                act_x_t(act, 1, t, scores_ps[1][:, t, :])
            act.wait_ge(s_kb, 16 * 3)
            act.wait_ge(s_tail[0], 16)
            nc.scalar.activation(kb_max[0:QROWS, :, :], kb_all[:, :, 0:KEYS], ACT.Copy).then_inc(kb_max_ready, 1)
            for e in range(HALVES):
                act_q_high(act, 1, e, scores_ps[0][:, e, :])
            copy_mask(1, pv16)
            act.wait_ge(s_tail[1], 16)
            nc.scalar.activation(kb_scores[0:QROWS, :, :], kb_all[:, :, 0:KEYS], ACT.Copy).then_inc(kb_scores_ready, 1)
            copy_weight(3, 4, scores_ps[1][:, 1, :])
            copy_mask(2, pv16)
            act_nm(act, 0, 0)
            for i in range(2):
                act.wait_ge(v_done, i + 1)
                act.wait_ge(v_ones, 1)
                nc.scalar.activation(v_all[0:KEYS, 2 * i:2 * i + 2, :, 0:DK],
                                     (pv_ps, work_ps)[i][0:KEYS, :].rearrange("k (b h d) -> k b h d", b=2, d=DK),
                                     ACT.Copy).then_inc(v_ready, 1)

            def body(b, first, last):
                for h in range(2):
                    n = 2 * b + h
                    apply_at = LAST_APPLY_AT if last and h == 1 else APPLY_AT
                    if not last and not first:
                        act_xs(act, n + 2)
                    for s in range(STEPS):
                        act.wait_ge(scores_done, PAIRS * n + s + 1)
                        if not (first and h == 0):
                            act.wait_ge(pv_done, 4 * (n - 1) + 2 * (s // 4) + 2)
                        nc.scalar.activation(probs[0:KEYS, s, :, :], scores_ps[s % 2][0:KEYS, :, :],
                                             ACT.Exp).then_inc(exp_done, 1)
                        if not last:
                            if s in XT_AT:
                                act_x_t(act, n + 2, XT_AT.index(s), work_ps)
                            if s in Q_AT:
                                act_q_high(act, n + 2, Q_AT.index(s), work_ps)
                        if s == NM_AT and not (last and h == 1):
                            act_nm(act, n + 1, 1 - h)
                        if first and h == 0 and s == 6:
                            copy_mask(3, work16)
                        for half in range(2):
                            if s == apply_at[half] and not first:
                                act_apply(act, n - 2, h, half)
                if first:
                    for m in range(4, BLOCKS):
                        act.wait_ge(s_x[m], 16)

            batches(act, body)
            for half in range(2):
                act_apply(act, BLOCKS - 2, 0, half, POOL_TILES)


        def dve_mask(dve, part):
            n, (t0, t1) = part + 1, (i * TILES for i in MASK_PARTS[part])
            dve.wait_ge(s_mask[max(i for i, (lo, _) in enumerate(MASK_LOADS) if lo <= MASK_PARTS[part][0])], 16)
            nc.vector.tensor_scalar(mask_eq[:, t0:t1, :], mask_all[:, t0:t1, :], 1.0, None, ALU.is_equal).then_inc(eq_ready, 1)
            dve.wait_ge(eq_ready, n)
            nc.vector.tensor_reduce(all_masked[:, t0:t1], mask_eq[:, t0:t1, :], AX.X, ALU.min).then_inc(full_ready, 1)
            dve.wait_ge(full_ready, n)
            nc.vector.tensor_scalar(not_full[:, t0:t1], all_masked[:, t0:t1], -1.0, 1.0, ALU.mult, ALU.add).then_inc(not_full_ready, 1)
            nc.vector.tensor_scalar(not_full_big[:, t0:t1], all_masked[:, t0:t1], -BIG, BIG, ALU.mult, ALU.add).then_inc(not_full_ready, 1)

        def dve_q_low(dve, m, e, bank):
            dve.wait_ge(q_high, HALVES * m + e + 1)
            nc.vector.tensor_tensor(q16[:, e, 1, :], bank[:, :], q16[:, e, 0, :], ALU.subtract).then_inc(q_low, 1)

        def dve_max(dve, m, u):
            (lo, hi), t = GROUPS[u // TILES], u % TILES
            dve.wait_ge(max_done, UNITS * m + u + 1)
            if u == 0 and not (isinstance(m, int) and m == 0):
                dve.wait_ge(nm_done, m)
            nc.vector.tensor_reduce(neg_max[:, t, lo:hi],
                                    max_ps[u % 2][:, 0:(hi - lo) * KEYS].rearrange("p (h k) -> p h k", k=KEYS),
                                    AX.X, ALU.max, negate=True).then_inc(max_reduced, 1)

        def dve_turn(dve, m, t, bank):
            dve.wait_ge(pv_done, 4 * m + t + 1)
            if not (isinstance(m, int) and m == 0 and t < 2):
                dve.wait_ge(ctx_normed, 4 * m + t - 1)
            nc.vector.transpose(ctx_q[:, t % 2, :, :], bank[:, :]).then_inc(pv_turned, 1)
            dve.wait_ge(pv_turned, 4 * m + t + 1)
            nc.vector.reciprocal(rden[:, t % 2, :], ctx_q[:, t % 2, :, DK]).then_inc(rden_ready, 1)

        def dve_ctx_e(dve, m, v, par):
            dve.wait_ge(ctx_normed, 4 * m + 2 * v + 2)
            nc.vector.transpose(ctx_e[par][:, v, :], ctx_n[:, v, :, :]).then_inc(ctx_e_ready, 1)

        def dve_residual(dve, m, rows, moves, half, product):
            dve.wait_ge(out_done, 2 * m + half + 1)
            if moves is not None:
                dve.wait_ge(*moves)
            nc.vector.tensor_tensor(rows[:, 2 * half:2 * half + 2, :], product,
                                    x_all[:, bass.ds(m * TILES + 2 * half, 2), :], ALU.add).then_inc(out_ready, 1)

        def dve_stats(dve, m, rows, t):
            if t > 0:
                dve.wait_ge(bn_ready, TILES * m + t)
            if t % 2 == 0:
                dve.wait_ge(out_ready, 2 * m + t // 2 + 1)
            nc.vector.bn_stats(bn[:, t, :], rows[:, t, :]).then_inc(bn_ready, 1)
            if t > 0:
                nc.vector.bn_aggr(mean_var[:, t - 1, :], bn[:, t - 1, :]).then_inc(mv_ready, 1)

        def dve_variance(dve, m):
            if isinstance(m, int) and m == BLOCKS - 1:
                dve.wait_ge(shift_ready, m)
            dve.wait_ge(bn_ready, TILES * (m + 1))
            dve.wait_ge(mv_ready, TILES * (m + 1) - 1)
            nc.vector.tensor_scalar(var_eps[:, 0:TILES - 1], mean_var[:, 0:TILES - 1, 1], EPS, None, ALU.add).then_inc(ve_ready, 1)
            nc.vector.bn_aggr(mean_var[:, TILES - 1, :], bn[:, TILES - 1, :]).then_inc(mv_ready, 1)
            dve.wait_ge(mv_ready, TILES * (m + 1))
            nc.vector.tensor_scalar(var_eps[:, TILES - 1:TILES], mean_var[:, TILES - 1:TILES, 1], EPS, None, ALU.add).then_inc(ve_ready, 1)
            nc.vector.tensor_scalar(neg_mean[:, :], mean_var[:, :, 0], -1.0, None, ALU.mult).then_inc(ve_ready, 1)

        def dve_scale(rows, t):
            return nc.vector.scalar_tensor_tensor(out=rows[:, t, :], in0=rows[:, t, :], scalar=neg_mean[:, t:t + 1],
                                                  in1=gamma_sb[:, :], op0=ALU.add, op1=ALU.mult)

        def dve_shift(rows, t):
            return nc.vector.scalar_tensor_tensor(out=rows[:, t, :], in0=rows[:, t, :], scalar=rstd[:, t:t + 1],
                                                  in1=beta_sb[:, :], op0=ALU.mult, op1=ALU.add)

        @block.vector
        def _(dve):
            nc.vector.memset(kb_tail[:, :, :], 1.0).then_inc(tail_ready, 1)
            dve.wait_ge(s_ident, 3)
            dve.wait_ge(tail_ready, 1)
            nc.vector.tensor_scalar(kb_tail[0:KEYS, 0, :], ident[0:KEYS, 0:KEYS], -BIG, None, ALU.mult).then_inc(tail_ready, 1)
            dve.wait_ge(tail_ready, 2)
            nc.vector.tensor_copy(kb_tail[0:KEYS, 1:HEADS, :],
                                  kb_tail[0:KEYS, 0, :].unsqueeze(1).to_broadcast([KEYS, HEADS - 1, KEYS])
                                  ).then_inc(tail_ready, 1)
            dve_mask(dve, 0)
            mask_product(nc.vector, dve, 0)
            for t in range(HALVES):
                dve.wait_ge(c_t_done, t + 1)
                nc.vector.tensor_copy(ctx_t[:, t, :], scores_ps[1][:, t, 0:BATCH * KEYS]).then_inc(c_t_ready, 1)
            for e in range(HALVES):
                dve.wait_ge(k_high, e + 1)
                nc.vector.scalar_tensor_tensor(out=k16[:, 1, e, :], in0=max_ps[e][:, 0:BATCH * KEYS],
                                               scalar=KSCALE, in1=k16[:, 0, e, :],
                                               op0=ALU.mult, op1=ALU.subtract).then_inc(k_low, 1)
                if e == 0:
                    dve.wait_ge(x_t_done, 2)
                    nc.vector.tensor_copy(x_t[:, 1, :], scores_ps[1][:, 0, :]).then_inc(x_t_ready, 1)
            dve_mask(dve, 1)
            mask_product(nc.vector, dve, 1)
            for e in range(HALVES):
                dve_q_low(dve, 0, e, (pv_ps, work_ps)[e])
            dve_mask(dve, 2)
            for u in range(UNITS):
                if u in (0, 2):
                    dve_q_low(dve, 1, u // 2, scores_ps[0][:, u // 2, :])
                dve_max(dve, 0, u)
            dve_mask(dve, 3)

            def body(b, first, last):
                for h in range(2):
                    n = 2 * b + h
                    for s in range(STEPS):
                        if s == Q_AT[0] + 1 and not last:
                            dve_q_low(dve, n + 2, 0, work_ps)
                        if not (last and h == 1):
                            for u in range(UNITS_AT[s]):
                                dve_max(dve, n + 1, UNIT_START[s] + u)
                        if s == Q_AT[1] + 1 and not last:
                            dve_q_low(dve, n + 2, 1, work_ps)
                        if s in CTX_AT and not (first and h == 0):
                            dve_ctx_e(dve, n - 1, CTX_AT.index(s), 1 - h)
                        if s in PV_AT[0:2] and not (first and h == 0):
                            dve_turn(dve, n - 1, 2 + PV_AT.index(s), pv_ps)
                        if s in PV_AT[2:4]:
                            dve_turn(dve, n, PV_AT.index(s) - 2, pv_ps)
                        if s == 6 and h == 0 and not last:
                            nc.vector.tensor_copy(kb_max[0:QROWS, :, :], kb_all[:, :, bass.ds((b + 1) * KEYS, KEYS)]
                                                  ).then_inc(kb_max_ready, 1)
                        if s == 7 and h == 1 and not last:
                            nc.vector.tensor_copy(kb_scores[0:QROWS, :, :], kb_all[:, :, bass.ds((b + 1) * KEYS, KEYS)]
                                                  ).then_inc(kb_scores_ready, 1)
                        if first and h == 0 and s == 6:
                            lo, hi = MASK_TURNS[4]
                            dve.wait_ge(mask_t_done, 5)
                            nc.vector.tensor_copy(mask_t[:, lo:hi, :], max16[1][0:KEYS, 0:(hi - lo) * BLOCK].rearrange(
                                "k (m q) -> k m q", q=BLOCK)).then_inc(mask_t_ready, 1)
                        if s == 7 and last and h == 1:
                            for t in range(2):
                                dve_stats(dve, n - 1, y[0], t)
                        if s in OUT_AT and not (first and h == 0):
                            moved = b
                            dve_residual(dve, n - 1, y[1 - h],
                                         None if isinstance(moved, int) and moved == 0 else (s_y[1 - h], 16 * moved),
                                         OUT_AT.index(s), work_ps[:, :].rearrange("p (t d) -> p t d", d=D))
                        if s in STATS_AT and not first:
                            dve_stats(dve, n - 2, y[h], STATS_AT.index(s))
                        if s == (LAST_VARIANCE_AT if last and h == 1 else VARIANCE_AT) and not first:
                            dve_variance(dve, n - 2)
                        if s == 3 and h == 0:
                            if not first:
                                dve.wait_ge(pv_done, 4 * n)
                            else:
                                dve.wait_ge(v_ready, 2)
                            nc.vector.tensor_copy(v_now[:, :, :], v_all[:, bass.ds(b, 1), :, :].rearrange("p a h k -> p (a h) k")
                                                  ).then_inc(v_now_ready, 1)
            batches(dve, body)
            dve.wait_ge(s_gb, 32)
            n = BLOCKS
            dve_turn(dve, n - 1, 2, pv_ps)
            dve_turn(dve, n - 1, 3, max_ps[0])
            dve_ctx_e(dve, n - 1, 0, 1)
            dve_ctx_e(dve, n - 1, 1, 1)
            for t in range(2, TILES):
                dve_stats(dve, n - 2, y[0], t)
            dve_variance(dve, n - 2)
            dve.wait_ge(ve_ready, 3 * (n - 1))
            dve_scale(y[0], POOL_TILES).then_inc(y_dve, 1)
            for half in range(2):
                dve_residual(dve, n - 1, xs, None, half, scores_ps[half][:, :, 0:D])
                if half == 0:
                    for t in range(2):
                        dve_stats(dve, n - 1, xs, t)
            dve.wait_ge(y_dve, 1)
            dve.wait_ge(rstd_ready, n - 1)
            dve_shift(y[0], POOL_TILES).then_inc(y_dve, 1)
            for t in range(2, TILES):
                dve_stats(dve, n - 1, xs, t)
            dve_variance(dve, n - 1)
            dve.wait_ge(ve_ready, 3 * n)
            for t in range(TILES):
                last = dve_scale(xs, t)
            last.then_inc(y_last, 1)
            dve.wait_ge(y_last, 1)
            dve.wait_ge(rstd_ready, n)
            for half in range(2):
                for t in range(2 * half, 2 * half + 2):
                    last = dve_shift(xs, t)
                last.then_inc(y_last, 1)

        def pe_scores(pe, m, s, par, b):
            if s == 0:
                pe.wait_ge(kb_scores_ready, b + 1)
                pe.wait_ge(s_nm, 16 * (m + 1))
            if not (isinstance(m, int) and m == 0 and s < 2):
                pe.wait_ge(exp_done, PAIRS * m + s - 1)
            for i in range(2):
                last = nc.tensor.matmul(scores_ps[s % 2][0:KEYS, i, :], kb_scores[:, 2 * s + i, :], R[par][:, 2 * s + i, :],
                                        start=True, stop=True)
            last.then_inc(scores_done, 1)

        def pe_max(pe, m, u, par, b):
            (lo, hi), t = GROUPS[u // TILES], u % TILES
            if u == 0:
                pe.wait_ge(kb_max_ready, b + 1)
            if t == 0:
                pe.wait_ge(s_R[par][u // TILES], 16 * RLOADS * (b + 1))
            if not (isinstance(m, int) and m == 0 and u < 2):
                pe.wait_ge(max_reduced, UNITS * m + u - 1)
            if u == 0 and not (isinstance(m, int) and m == 0):
                pe.wait_ge(nm_ready, m)
            for i in range(hi - lo):
                last = nc.tensor.matmul(max_ps[u % 2][:, i * KEYS:(i + 1) * KEYS],
                                        R[par][0:MAX_ROW, lo + i, t * P:(t + 1) * P], kb_max[0:MAX_ROW, lo + i, :],
                                        start=True, stop=True)
            last.then_inc(max_done, 1)

        def pe_nm(pe, m):
            pe.wait_ge(max_reduced, UNITS * (m + 1))
            for t in range(TILES):
                last = nc.tensor.transpose(max16[0][0:HEADS, t * P:(t + 1) * P], neg_max[:, t, :], ident16[:, :])
            last.then_inc(nm_done, 1)

        def pe_pv(pe, m, t, batches_ready, bank):
            v, u = t // 2, t % 2
            if t == 0:
                pe.wait_ge(v_now_ready, batches_ready)
            pe.wait_ge(exp_done, PAIRS * m + 4 * (v + 1))
            if bank is pv_ps and not (isinstance(m, int) and m == 0 and t == 0):
                pe.wait_ge(pv_turned, 4 * m + t)
            for j in range(4):
                last = nc.tensor.matmul(bank[32 * j:32 * (j + 1), :], v_now[:, 8 * v + 2 * j + u, :],
                                        probs[:, 4 * v + j, u, :], start=True, stop=True)
            last.then_inc(pv_done, 1)

        def pe_mask_t(pe, lo, hi, bank):
            for t in range(lo * TILES, hi * TILES):
                c = (t - lo * TILES) * P
                last = nc.tensor.transpose(bank[0:KEYS, c:c + P], mask16[:, t, :], ident16[:, :])
            last.then_inc(mask_t_done, 1)

        def pe_x_t(pe, m, d, bank):
            if d == 0:
                pe.wait_ge(xs_ready, TILES * (m + 1))
            for t in range(TILES):
                last = nc.tensor.transpose(bank[:, t * P:(t + 1) * P], xs[:, t, d * P:(d + 1) * P], ident[:, :])
            last.then_inc(x_t_done, 1)

        def pe_q(pe, m, e, bank):
            pe.wait_ge(x_t_ready, HALVES * (m + 1))
            for t in range(HALVES):
                last = nc.tensor.matmul(bank[:, :], w_t[0][:, t, e * P:(e + 1) * P], x_t[:, t, :],
                                        start=(t == 0), stop=(t == HALVES - 1))
            last.then_inc(q_done, 1)

        def pe_out(pe, m, par, half, bank):
            if half == 0:
                pe.wait_ge(ctx_e_ready, HALVES * (m + 1))
            for i in range(2):
                q0 = (2 * half + i) * P
                for v in range(HALVES):
                    last = nc.tensor.matmul(bank[:, i * D:(i + 1) * D], ctx_e[par][:, v, q0:q0 + P], w_t[3][:, v, :],
                                            start=(v == 0), stop=(v == HALVES - 1))
            last.then_inc(out_done, 1)

        @block.tensor
        def _(pe):
            def turn_weight(i, bank):
                pe.wait_ge(s_w[i] if i < 3 else s_y[1], 16)
                for t in range(HALVES):
                    for e in range(HALVES):
                        last = nc.tensor.transpose(bank[:, t * D + e * P:t * D + (e + 1) * P],
                                                   w_in[i][:, e, t * P:(t + 1) * P], ident[:, :])
                last.then_inc(w_t_done, 1)

            pe.wait_ge(s_ident, 3)
            turn_weight(1, scores_ps[0][:, 0, :])
            pe.wait_ge(s_ctx, 16)
            for t in range(HALVES):
                for b in range(BATCH):
                    last = nc.tensor.transpose(scores_ps[1][:, t, b * KEYS:(b + 1) * KEYS], ctx_sb[:, b, t * P:(t + 1) * P],
                                               ident[0:KEYS, 0:KEYS])
                last.then_inc(c_t_done, 1)
            turn_weight(0, scores_ps[0][:, 1, :])
            pe.wait_ge(mask16_ready, 1)
            pe_mask_t(pe, *MASK_TURNS[0], work16)
            pe.wait_ge(c_t_ready, HALVES)
            pe.wait_ge(w_t_ready, 1)
            for e in range(HALVES):
                for t in range(HALVES):
                    last = nc.tensor.matmul(max_ps[e][:, 0:BATCH * KEYS], w_t[1][:, t, e * P:(e + 1) * P],
                                            ctx_t[:, t, :], start=(t == 0), stop=(t == HALVES - 1))
                last.then_inc(k_done, 1)
                if e == 0:
                    for t in range(HALVES):
                        pe_x_t(pe, 0, t, scores_ps[t][:, 0, :])
            pe.wait_ge(w_t_ready, 2)
            pe.wait_ge(mask_t_ready, 1)
            for e in range(HALVES):
                pe_q(pe, 0, e, (pv_ps, work_ps)[e])
            pe.wait_ge(k_low, HALVES)
            turn_weight(2, max_ps[0][:, :])
            for t in range(HALVES):
                pe_x_t(pe, 1, t, scores_ps[1][:, t, :])
            for e in range(HALVES):
                pe_q(pe, 1, e, scores_ps[0][:, e, :])
            pe.wait_ge(q_low, HALVES)
            pe.wait_ge(mask16_ready, 2)
            pe_mask_t(pe, *MASK_TURNS[1], pv16)
            pe.wait_ge(w_t_ready, 3)
            for u in range(UNITS):
                pe_max(pe, 0, u, 0, 0)
                if u == WO_U:
                    pe.wait_ge(x_t_ready, 2 * HALVES)
                    turn_weight(3, scores_ps[1][:, 1, :])
                if u == MASK_U:
                    pe.wait_ge(mask16_ready, 3)
                    pe.wait_ge(mask_t_ready, 2)
                    pe_mask_t(pe, *MASK_TURNS[2], pv16)
            pe_nm(pe, 0)
            pe.wait_ge(mask_t_ready, 3)
            for b in range(BATCH):
                for t in range(HALVES):
                    last = nc.tensor.matmul((pv_ps, work_ps)[b // 2][0:KEYS, (b % 2) * D:(b % 2 + 1) * D],
                                            ctx_t[:, t, b * KEYS:(b + 1) * KEYS],
                                            w_t[2][:, t, :], start=(t == 0), stop=(t == HALVES - 1))
                if b % 2 == 1:
                    last.then_inc(v_done, 1)
            pe.wait_ge(w_t_ready, 4)
            pe.wait_ge(q_low, 2 * HALVES)
            pe.wait_ge(s_zero, 1 + 6)

            def body(b, first, last):
                for h in range(2):
                    n = 2 * b + h
                    for s in range(STEPS):
                        if first and h == 0 and s == 6:
                            pe.wait_ge(s_zero, 1 + PAIRS)
                        pe_scores(pe, n, s, h, b)
                        if first and h == 1 and s == 0:
                            pe.wait_ge(mask_t_ready, len(MASK_TURNS))
                        if not (last and h == 1):
                            for u in range(UNITS_AT[s]):
                                pe_max(pe, n + 1, UNIT_START[s] + u, 1 - h, b + h)
                        if s in PV_AT[0:2] and not (first and h == 0):
                            pe_pv(pe, n - 1, 2 + PV_AT.index(s), b, pv_ps)
                        if s in PV_AT[2:4]:
                            pe_pv(pe, n, PV_AT.index(s) - 2, b + 1, pv_ps)
                        if s == NM_AT and not (last and h == 1):
                            pe_nm(pe, n + 1)
                        if not last:
                            if s == XT_AT[0]:
                                if first and h == 0:
                                    pe.wait_ge(v_ready, 2)
                                elif not first:
                                    pe.wait_ge(out_ready, 2 * (n - 1))
                                pe_x_t(pe, n + 2, 0, work_ps)
                            if s == XT_AT[1]:
                                pe.wait_ge(x_t_ready, HALVES * (n + 2) + 1)
                                pe_x_t(pe, n + 2, 1, work_ps)
                            if s == Q_AT[0]:
                                pe_q(pe, n + 2, 0, work_ps)
                            if s == Q_AT[1]:
                                pe.wait_ge(q_low, HALVES * (n + 2) + 1)
                                pe_q(pe, n + 2, 1, work_ps)
                        if first and h == 0 and s == 6:
                            pe.wait_ge(mask16_ready, 4)
                            pe.wait_ge(q_low, 3 * HALVES)
                            pe_mask_t(pe, *MASK_TURNS[3], work16)
                            pe_mask_t(pe, *MASK_TURNS[4], max16[1])
                        if s == OUT_AT[0] and not (first and h == 0):
                            if not last:
                                pe.wait_ge(q_low, HALVES * (n + 3))
                            else:
                                pe.wait_ge(out_ready, 2 * (n - 1))
                            pe_out(pe, n - 1, 1 - h, 0, work_ps)
                        if s == OUT_AT[1] and not (first and h == 0):
                            pe.wait_ge(out_ready, 2 * (n - 1) + 1)
                            pe_out(pe, n - 1, 1 - h, 1, work_ps)

            batches(pe, body)
            n = BLOCKS
            pe_pv(pe, n - 1, 2, BATCH, pv_ps)
            pe_pv(pe, n - 1, 3, BATCH, max_ps[0])
            pe.wait_ge(exp_done, PAIRS * n)
            for v in range(HALVES):
                pe.wait_ge(ctx_e_ready, HALVES * (n - 1) + v + 1)
                for t in range(TILES):
                    last = nc.tensor.matmul(scores_ps[t // 2][:, t % 2, 0:D],
                                            ctx_e[1][:, v, t * P:(t + 1) * P], w_t[3][:, v, :], start=(v == 0), stop=(v == 1))
                    if v == 1 and t % 2 == 1:
                        last.then_inc(out_done, 1)


_INS = ['x', 'ctx_1024', 'mask_BxSxS2_ik1', 'L0_xattn_W_Q', 'L0_xattn_W_K', 'L0_xattn_W_V', 'L0_xattn_W_O',
        'L0_xattn_gamma', 'L0_xattn_beta']


def kernel(**inputs):
    import numpy as np
    import concourse.bacc as bacc
    from concourse.bass_utils import run_bass_kernel_spmd

    nc = bacc.Bacc("TRN2", target_bir_lowering=False, num_devices=1)
    arrays, args = {}, []
    for name in _INS:
        a = np.ascontiguousarray(inputs[name])
        arrays[f"in_{name}"] = a
        args.append(nc.dram_tensor(f"in_{name}", a.shape, mybir.dt.from_np(a.dtype), kind="ExternalInput").ap())
    out = nc.dram_tensor("out", (BATCH, SEQ, D), F32, kind="ExternalOutput").ap()
    cross_attention(nc, *args, out)
    return run_bass_kernel_spmd(nc, [arrays], core_ids=[0]).results[0]["out"]
```
